# Optimizing a Trainium2 kernel written in Bass

```python
import numpy as np
import jax
import jax.numpy as jnp

def _softmax(x, axis=-1):
    return jax.nn.softmax(x, axis=axis)

def _gelu(x):
    return jax.nn.gelu(x, approximate=True)

def _silu(x):
    return jax.nn.silu(x)

def _sigmoid(x):
    return jax.nn.sigmoid(x)

def _layernorm(x, axis=-1, eps=1e-05):
    m = jnp.mean(x, axis=axis, keepdims=True)
    v = jnp.var(x, axis=axis, keepdims=True)
    return (x - m) / jnp.sqrt(v + eps)

def _scatter_add(tgt, idx, src, axis=0):
    return tgt.at[idx].add(src)

def _segment_sum(src, seg, n):
    return jax.ops.segment_sum(src, seg, n)
kernel_name = 'mk_audio_tower_d1_tok_aud1d512_r4_cd9c0c'

def setup_inputs(seed: int=0):
    np.random.seed(seed)
    _w = jnp.asarray

    def _rec_inputs():
        import jax
        import jax.numpy as jnp
        _rk = jax.random.key(seed)
        x = -0.000928989 + 1.00043 * jax.random.normal(jax.random.fold_in(_rk, 1), (4, 20000), jnp.float32)
        return x
    x = _rec_inputs()

    def _L0_tok_setup():
        import jax, jax.numpy as jnp
        import numpy as np
        SEG_LEN = 48
        STRIDE = SEG_LEN // 2
        CURVATURE = 1.0
        BALL_EPS = 0.004
        MIN_NORM = 1e-15
        key = jax.random.key(seed)
        k1, k2, k3 = jax.random.split(key, 3)
        B, L, D = (128, 2048, 128)
        x_raw = jax.random.normal(k1, (B, L), dtype=jnp.float32)
        W = jax.random.normal(k2, (SEG_LEN, D), dtype=jnp.float32) * (1.0 / np.sqrt(SEG_LEN))
        b = jax.random.normal(k3, (D,), dtype=jnp.float32) * 0.01
        effective_scale = jnp.ones((1,), dtype=jnp.float32)
        return {'x_raw': x_raw, 'W': W, 'b': b, 'effective_scale': effective_scale}
    _L0_tok_all = _L0_tok_setup()
    _L0_tok_in = {k: v for k, v in _L0_tok_all.items() if k in ('W', 'b', 'effective_scale')}
    del _L0_tok_all

    def _L0_attn_setup():
        import jax, jax.numpy as jnp
        import numpy as np
        SIZE = 128
        B, S = (8, 512)

        def _fourier_filter(xf, real, imag):
            w = real.astype(xf.dtype) + 1j * imag.astype(xf.dtype)
            return jnp.fft.ifft(xf * w[None, None, :], axis=-1).real
        key = jax.random.key(seed)
        kx, = jax.random.split(key, 1)
        x = jax.random.normal(kx, (B, S, SIZE), dtype=jnp.float32)
        return {'x': x, 'q_real': jnp.ones((SIZE,), jnp.float32), 'q_imag': jnp.zeros((SIZE,), jnp.float32), 'k_real': jnp.ones((SIZE,), jnp.float32), 'k_imag': jnp.zeros((SIZE,), jnp.float32), 'v_real': jnp.ones((SIZE,), jnp.float32), 'v_imag': jnp.zeros((SIZE,), jnp.float32)}
    _L0_attn_all = _L0_attn_setup()
    _L0_attn_in = {k: v for k, v in _L0_attn_all.items() if k in ('q_real', 'q_imag', 'k_real', 'k_imag', 'v_real', 'v_imag')}
    del _L0_attn_all

    def _L0_ffn_setup():
        import jax, jax.numpy as jnp
        import numpy as np
        TOP_K = 2
        key = jax.random.key(seed)
        ks = jax.random.split(key, 6)
        B, T, C, E, H = (4, 1024, 128, 8, 512)
        x = jax.random.normal(ks[0], (B, T, C), dtype=jnp.float32)
        W_router = jax.random.normal(ks[1], (C, E), dtype=jnp.float32) * 0.02
        W1 = jax.random.normal(ks[2], (E, C, H), dtype=jnp.float32) * 0.02
        b1 = jnp.zeros((E, H), dtype=jnp.float32)
        W2 = jax.random.normal(ks[3], (E, H, C), dtype=jnp.float32) * 0.02
        b2 = jnp.zeros((E, C), dtype=jnp.float32)
        return {'x': x, 'W_router': W_router, 'W1': W1, 'b1': b1, 'W2': W2, 'b2': b2}
    _L0_ffn_all = _L0_ffn_setup()
    _L0_ffn_in = {k: v for k, v in _L0_ffn_all.items() if k in ('W_router', 'W1', 'b1', 'W2', 'b2')}
    del _L0_ffn_all
    return {'x': x, 'L0_tok_W': _L0_tok_in['W'], 'L0_tok_b': _L0_tok_in['b'], 'L0_tok_effective_scale': _L0_tok_in['effective_scale'], 'L0_attn_q_real': _L0_attn_in['q_real'], 'L0_attn_q_imag': _L0_attn_in['q_imag'], 'L0_attn_k_real': _L0_attn_in['k_real'], 'L0_attn_k_imag': _L0_attn_in['k_imag'], 'L0_attn_v_real': _L0_attn_in['v_real'], 'L0_attn_v_imag': _L0_attn_in['v_imag'], 'L0_ffn_W_router': _L0_ffn_in['W_router'], 'L0_ffn_W1': _L0_ffn_in['W1'], 'L0_ffn_b1': _L0_ffn_in['b1'], 'L0_ffn_W2': _L0_ffn_in['W2'], 'L0_ffn_b2': _L0_ffn_in['b2']}

def reference(x, L0_tok_W, L0_tok_b, L0_tok_effective_scale, L0_attn_q_real, L0_attn_q_imag, L0_attn_k_real, L0_attn_k_imag, L0_attn_v_real, L0_attn_v_imag, L0_ffn_W_router, L0_ffn_W1, L0_ffn_b1, L0_ffn_W2, L0_ffn_b2):
    import jax
    import jax.numpy as jnp

    def _L0_tok_ref(x_raw, W, b, effective_scale):
        import jax, jax.numpy as jnp
        import numpy as np
        SEG_LEN = 48
        STRIDE = SEG_LEN // 2
        CURVATURE = 1.0
        BALL_EPS = 0.004
        MIN_NORM = 1e-15
        B, L = x_raw.shape
        seg_len, D = W.shape
        N = (L - seg_len) // STRIDE + 1
        idx = jnp.arange(N)[:, None] * STRIDE + jnp.arange(seg_len)[None, :]
        segs = x_raw[:, idx]
        z = jnp.einsum('bnl,ld->bnd', segs, W) + b
        scale = jnp.tanh(effective_scale[0])
        u = z * scale
        sqrt_c = jnp.sqrt(jnp.float32(CURVATURE))
        u_norm = jnp.maximum(jnp.linalg.norm(u, axis=-1, keepdims=True), MIN_NORM)
        y = jnp.tanh(sqrt_c * u_norm) * u / (sqrt_c * u_norm)
        y_norm = jnp.maximum(jnp.linalg.norm(y, axis=-1, keepdims=True), MIN_NORM)
        maxnorm = (1.0 - BALL_EPS) / sqrt_c
        y = jnp.where(y_norm > maxnorm, y / y_norm * maxnorm, y)
        return y

    def _L0_attn_ref(x, q_real, q_imag, k_real, k_imag, v_real, v_imag):
        import jax, jax.numpy as jnp
        import numpy as np
        SIZE = 128
        B, S = (8, 512)

        def _fourier_filter(xf, real, imag):
            w = real.astype(xf.dtype) + 1j * imag.astype(xf.dtype)
            return jnp.fft.ifft(xf * w[None, None, :], axis=-1).real
        xf = jnp.fft.fft(x, axis=-1)
        q = _fourier_filter(xf, q_real, q_imag).astype(x.dtype)
        k = _fourier_filter(xf, k_real, k_imag).astype(x.dtype)
        v = _fourier_filter(xf, v_real, v_imag).astype(x.dtype)
        scale = np.sqrt(SIZE).astype(np.float32)
        attn = jnp.einsum('bsd,btd->bst', q, k) / scale
        attn = jax.nn.softmax(attn, axis=-1)
        return jnp.einsum('bst,btd->bsd', attn, v)

    def _L0_ffn_ref(x, W_router, W1, b1, W2, b2):
        import jax, jax.numpy as jnp
        import numpy as np
        TOP_K = 2
        B, T, C = x.shape
        E = W_router.shape[1]
        x_flat = x.reshape(B * T, C)
        logits = x_flat @ W_router
        probs = jax.nn.softmax(logits, axis=-1)
        topk_p, topk_i = jax.lax.top_k(probs, TOP_K)
        topk_p = topk_p / topk_p.sum(axis=-1, keepdims=True)
        combine = (jax.nn.one_hot(topk_i, E, dtype=x_flat.dtype) * topk_p[..., None]).sum(axis=1)
        out = jnp.zeros_like(x_flat)
        for e in range(E):
            h = jax.nn.relu(x_flat @ W1[e] + b1[e])
            y = h @ W2[e] + b2[e]
            out = out + combine[:, e:e + 1] * y
        return out.reshape(B, T, C)
    h = _L0_tok_ref(x, L0_tok_W, L0_tok_b, L0_tok_effective_scale)
    h = h + _L0_attn_ref(_layernorm(h, axis=-1), L0_attn_q_real, L0_attn_q_imag, L0_attn_k_real, L0_attn_k_imag, L0_attn_v_real, L0_attn_v_imag)
    h = h + _L0_ffn_ref(_layernorm(h, axis=-1), L0_ffn_W_router, L0_ffn_W1, L0_ffn_b1, L0_ffn_W2, L0_ffn_b2)
    return h

_drawn_inputs = setup_inputs


def setup_inputs(seed=0):
    import zlib

    import numpy as np

    out = dict(_drawn_inputs(seed))
    spreads = {'L0_attn_q_real': (1.0, 0.6),
     'L0_attn_q_imag': (0.0, 2.0),
     'L0_attn_k_real': (1.0, 0.6),
     'L0_attn_k_imag': (0.0, 2.0),
     'L0_attn_v_real': (1.0, 0.2),
     'L0_attn_v_imag': (0.0, 0.1),
     'L0_ffn_b1': (0.0, 0.42),
     'L0_ffn_b2': (0.0, 0.1)}
    factors = {'L0_tok_b': 4.586}
    for name, (base, spread) in spreads.items():
        noise = np.random.default_rng([zlib.crc32(name.encode()), seed]).standard_normal(out[name].shape)
        drawn = base * np.exp(spread * noise) if base else spread * noise
        out[name] = jnp.asarray(drawn.astype(out[name].dtype))
    for name, factor in factors.items():
        out[name] = (out[name] * factor).astype(out[name].dtype)
    return out
```

```python
from contextlib import ExitStack

import numpy as np

import concourse.bass as bass
from concourse import mybir

F32 = mybir.dt.float32
F16 = mybir.dt.float16
I32 = mybir.dt.int32
ALU = mybir.AluOpType
ACT = mybir.ActivationFunctionType
AX = mybir.AxisListType.X

P = 128
B, L = 4, 20000
SEG, STRIDE = 48, 24
N = (L - SEG) // STRIDE + 1
T = -(-N // P)
LAST = N - (T - 1) * P
NP = T * P
KH = N // 2
E, H = 8, 512
HC = H // P
K = SEG + 1
EPS_LN = 1e-5
MIN_NORM = 1e-15
MAX_NORM = 1.0 - 0.004
BIG = 2.0 ** 100


def build(nc, x, wb, scale1, tables, filters, wr, w1, b1t, w2, b2, out):
    ctx = ExitStack()
    with ctx:
        def sb(name, shape, dt=F32):
            return ctx.enter_context(nc.sbuf_tensor(name, shape, dt))

        def sem(name):
            return ctx.enter_context(nc.semaphore(name))

        ps = ctx.enter_context(nc.psum_tensor("ps", [P, 8, 512], F32))

        def banks(b, cols):
            return ps[:, b:b + -(-cols // 512), :].rearrange("p b c -> p (b c)")[:, 0:cols]

        tab = sb("tab", [P, 4 * P])
        cos_t, sin_t, ident = tab[:, 0:P], tab[:, P:2 * P], tab[:, 2 * P:3 * P]
        identh = sb("identh", [P, P], F16)
        filt = sb("filt", [P, 6])
        wb_sb = sb("wb_sb", [K, P])
        sc_in = sb("sc_in", [P, 1])
        wr_sb = sb("wr_sb", [P, E])
        w1_sb = sb("w1_sb", [P, E * H])
        w2_sb = sb("w2_sb", [P, E * H])
        b1_sb = sb("b1_sb", [P, E * HC])
        b2_sb = sb("b2_sb", [1, E * P])
        fa = sb("fa", [P, 3, P])
        fb = sb("fb", [P, 3, P])
        fneg = sb("fneg", [P, 3])
        cqk = sb("cqk", [P, 2, P])
        g32 = sb("g32", [P, P])
        cv32 = sb("cv32", [P, P])
        gh, gl = sb("gh", [P, P], F16), sb("gl", [P, P], F16)
        cvh, cvl = sb("cvh", [P, P], F16), sb("cvl", [P, P], F16)
        wrh, wrl = sb("wrh", [P, E], F16), sb("wrl", [P, E], F16)
        w1h, w1l = sb("w1h", [P, E * H], F16), sb("w1l", [P, E * H], F16)
        w2h, w2l = sb("w2h", [P, E * H], F16), sb("w2l", [P, E * H], F16)
        nb1 = sb("nb1", [P, E * HC])
        rev8 = sb("rev8", [P, E])
        mx_part, mx_all = sb("mx_part", [P, 8]), sb("mx_all", [P, 8])
        sc2, inv2 = sb("sc2", [P, 8]), sb("inv2", [P, 8])
        inv_s, inv12 = sb("inv_s", [P, 1]), sb("inv12", [P, 1])
        crow = sb("crow", [1, E * P])
        onesrow = sb("onesrow", [1, P])
        cbc = sb("cbc", [P, E * P])

        seg = sb("seg", [P, 2, T, K])
        segT = sb("segT", [K, NP])
        h = sb("h", [P, B * T, P])
        zmv = sb("zmv", [P, B * T, 2])
        bst = sb("bst", [P, T, 6])
        f = sb("f", [P, B * T])
        frs = sb("frs", [P, B * T])
        tmp = sb("tmp", [P, 4, B * T])
        half_c, mhalf_c = sb("half_c", [P, B * T]), sb("mhalf_c", [P, B * T])
        th = sb("th", [P, 1])
        xn = sb("xn", [P, T, P])
        xTh, xTl = sb("xTh", [P, B * NP], F16), sb("xTl", [P, B * NP], F16)
        yTh, yTl = sb("yTh", [P, B * NP], F16), sb("yTl", [P, B * NP], F16)
        v32 = sb("v32", [P, B * T, P])
        prob = sb("prob", [P, 2, NP])
        probT = sb("probT", [P, NP])
        nmax, nbias, rsum, rinv = (sb(n, [P, 2]) for n in ("nmax", "nbias", "rsum", "rinv"))
        st6 = sb("st6", [P, 2, 6])
        h2mv = sb("h2mv", [P, B * T, 2])
        x2h, x2l = sb("x2h", [P, NP], F16), sb("x2l", [P, NP], F16)
        x2Th, x2Tl = sb("x2Th", [P, B * NP], F16), sb("x2Tl", [P, B * NP], F16)
        lg = sb("lg", [P, B * T, E])
        lg2, eq, cand, m1h, m2h = (sb(n, [P, B * T, E]) for n in ("lg2", "eq", "cand", "m1h", "m2h"))
        r1 = sb("r1", [P, 6, B * T])
        comb = sb("comb", [P, B * T, E])
        hu = sb("hu", [P, 2, H])
        huh, hul = sb("huh", [P, 2, H], F16), sb("hul", [P, 2, H], F16)
        yv = sb("yv", [P, 2, P])

        (ld_tab, ld_wb, ld_filt, ld_w, st_out) = map(sem, ("ld_tab", "ld_wb", "ld_filt", "ld_w", "st_out"))
        ld_seg = sem("ld_seg")
        (filt_ready, filt_mm, filt_cp, mx_ready, mx_red, scales_ready, splits_ready, ident_ready,
         c_mm, c_row, c_bc, c_ready, pool_c, ones_seg) = map(sem, (
             "filt_ready", "filt_mm", "filt_cp", "mx_ready", "mx_red", "scales_ready", "splits_ready",
             "ident_ready", "c_mm", "c_row", "c_bc", "c_ready", "pool_c", "ones_seg"))
        (segT_mm, segT_ready, z_mm, z_ready, zst_ready, f_pow, f_pow_done, f_tanh, f_ready, xn_ready, xT_mm,
         xTh_ready, xTl_ready, y_mm, yh_ready, yl_ready, v_mm, v_ready, h_ready) = map(sem, (
             "segT_mm", "segT_ready", "z_mm", "z_ready", "zst_ready", "f_pow", "f_pow_done", "f_tanh", "f_ready", "xn_ready",
             "xT_mm", "xTh_ready", "xTl_ready", "y_mm", "yh_ready", "yl_ready", "v_mm", "v_ready",
             "h_ready"))
        (s_mm, nb_ready, p_ready, pT_mm, pTa_ready, pTb_ready, o_mm, o_used) = map(sem, (
            "s_mm", "nb_ready", "p_ready", "pT_mm", "pTa_ready", "pTb_ready", "o_mm", "o_used"))
        (rs2_in, rs2_ready, x2_ready, x2h_ready, x2l_ready, x2T_mm, x2T_ready, lg_mm, lg_ready, d_ready,
         e_ready, comb_ready) = map(sem, (
             "rs2_in", "rs2_ready", "x2_ready", "x2h_ready", "x2l_ready", "x2T_mm", "x2T_ready", "lg_mm",
             "lg_ready", "d_ready", "e_ready", "comb_ready"))
        (h_mm, hu_ready, huh_ready, hul_ready, y2_mm, yv_ready, acc_done) = map(sem, (
            "h_mm", "hu_ready", "huh_ready", "hul_ready", "y2_mm", "yv_ready", "acc_done"))

        C_G, C_V, C_R, C_1, C_2, C_B = range(6)

        block = ctx.enter_context(nc.Block())

        @block.sync
        def _(sp):
            sp.dma_start(tab[:], tables).then_inc(ld_tab, 16)
            sp.dma_start(filt[:], filters).then_inc(ld_filt, 16)
            sp.dma_start(wb_sb[:], wb).then_inc(ld_wb, 16)
            sp.dma_start(sc_in[:], scale1).then_inc(ld_wb, 16)
            for b in range(B):
                if b == 0:
                    sp.wait_ge(ones_seg, 1)
                if b == 2:
                    for dst, src in ((wr_sb, wr), (b1_sb, b1t), (b2_sb, b2), (w1_sb, w1), (w2_sb, w2)):
                        sp.dma_start(dst[:], src).then_inc(ld_w, 16)
                if b >= 2:
                    sp.wait_ge(segT_mm, b - 1)
                sp.dma_start(seg[:, b % 2, 0:T - 1, 0:SEG],
                             bass.AP(tensor=x.tensor, offset=b * L,
                                     ap=[[STRIDE, P], [STRIDE * P, T - 1], [1, SEG]])).then_inc(ld_seg, 16)
                sp.dma_start(seg[0:LAST, b % 2, T - 1, 0:SEG],
                             bass.AP(tensor=x.tensor, offset=b * L + STRIDE * P * (T - 1),
                                     ap=[[STRIDE, LAST], [1, SEG]])).then_inc(ld_seg, 16)
                sp.wait_ge(ld_seg, 32 * (b + 1))
            sp.wait_ge(acc_done, E * B * T)
            for b in range(B):
                sp.dma_start(out[b, 0:N - LAST, :].rearrange("(i p) d -> p i d", p=P),
                             h[:, b * T:b * T + T - 1, :]).then_inc(st_out, 16)
                sp.dma_start(out[b, N - LAST:N, :], h[0:LAST, b * T + T - 1, :]).then_inc(st_out, 16)
            sp.wait_ge(st_out, 32 * B)

        @block.gpsimd
        def _(pool):
            pool.memset(seg[:], 0.0)
            pool.drain()
            pool.memset(seg[:, :, :, SEG:K], 1.0).then_inc(ones_seg, 1)
            pool.memset(half_c[:], 0.5)
            pool.memset(mhalf_c[:], -0.5)
            pool.memset(onesrow[:], 1.0)
            pool.memset(prob[:, :, N:NP], 0.0)
            pool.memset(mx_part[:], 0.0)
            pool.iota(rev8[:], pattern=[[-1, E]], base=E, channel_multiplier=0,
                      allow_small_or_imprecise_dtypes=True).then_inc(pool_c, 1)
            pool.wait_ge(mx_ready, 1)
            pool.partition_all_reduce(mx_all[:], mx_part[:], P, bass.bass_isa.ReduceOp.max).then_inc(mx_red, 1)
            pool.wait_ge(f_pow, 1)
            pool.tensor_tensor(tmp[:, 1, :], tmp[:, 0, :], half_c[:], ALU.pow).then_inc(f_pow_done, 1)
            pool.wait_ge(f_pow, 2)
            pool.tensor_tensor(tmp[:, 1, :], tmp[:, 0, :], mhalf_c[:], ALU.pow).then_inc(f_pow_done, 1)
            pool.wait_ge(rs2_in, 1)
            pool.tensor_tensor(tmp[:, 1, :], tmp[:, 0, :], mhalf_c[:], ALU.pow).then_inc(rs2_ready, 1)

        @block.scalar
        def _(act):
            act.wait_ge(ld_wb, 32)
            nc.scalar.activation(th[:], sc_in[:], ACT.Tanh).then_inc(f_tanh, 1)
            for b in range(B):
                act.wait_ge(segT_mm, b + 1)
                if b:
                    act.wait_ge(z_mm, b)
                nc.scalar.copy(segT[:], banks(0, NP)[0:K, :]).then_inc(segT_ready, 1)
                act.wait_ge(z_mm, b + 1)
                nc.scalar.copy(h[:, b * T:b * T + T, :].rearrange("p t d -> p (t d)"),
                               banks(2, NP)).then_inc(z_ready, 1)
            act.wait_ge(f_tanh, 2)
            nc.scalar.activation(tmp[:, 2, :], tmp[:, 1, :], ACT.Tanh).then_inc(f_tanh, 1)
            act.wait_ge(splits_ready, 1)
            for b in range(B):
                cols = slice(b * NP, (b + 1) * NP)
                act.wait_ge(xT_mm, b + 1)
                nc.scalar.copy(xTh[:, cols], banks(4, NP)).then_inc(xTh_ready, 1)
                act.wait_ge(y_mm, b + 1)
                nc.scalar.copy(yTh[:, cols].rearrange("p (k c) -> p k c", k=2),
                               ps[:, 6:8, 0:NP // 2]).then_inc(yh_ready, 1)
                act.wait_ge(v_mm, b + 1)
                nc.scalar.activation(v32[:, b * T:b * T + T, :].rearrange("p t d -> p (t d)"), banks(0, NP),
                                     ACT.Copy, scale=inv2[:, C_V:C_V + 1]).then_inc(v_ready, 1)
            for t in range(B * T):
                u = t % 2
                act.wait_ge(nb_ready, t + 1)
                if t >= 2:
                    act.wait_ge(pT_mm, t - 1)
                nc.scalar.activation(prob[:, u, 0:N].rearrange("p (k c) -> p k c", k=2),
                                     ps[:, 2 * u:2 * u + 2, 0:KH], ACT.Exp, bias=nbias[:, u:u + 1],
                                     scale=inv_s[:], accum_out=rsum[:, u:u + 1]).then_inc(p_ready, 1)
                act.wait_ge(pT_mm, t + 1)
                if t >= 1:
                    act.wait_ge(o_mm, t)
                nc.scalar.copy(probT[:, 0:512], ps[:, 4, :]).then_inc(pTa_ready, 1)
            for b in range(B):
                cols = slice(b * NP, (b + 1) * NP)
                act.wait_ge(x2_ready, b + 1)
                if b:
                    act.wait_ge(x2T_mm, b)
                nc.scalar.copy(x2h[:], xn[:].rearrange("p t d -> p (t d)")).then_inc(x2h_ready, 1)
                act.wait_ge(x2T_mm, b + 1)
                nc.scalar.copy(x2Th[:, cols], banks(0, NP // 2).bitcast(F16)).then_inc(x2T_ready, 1)
                act.wait_ge(lg_mm, b + 1)
                nc.scalar.copy(lg[:, b * T:b * T + T, :].rearrange("p t e -> p (t e)"),
                               ps[:, 2, 0:T * E]).then_inc(lg_ready, 1)
            act.wait_ge(d_ready, 1)
            nc.scalar.activation(r1[:, 5, :], r1[:, 4, :], ACT.Exp, scale=inv2[:, C_R:C_R + 1]).then_inc(e_ready, 1)
            with act.Fori(0, E * B * T // 2) as i:
                for u in range(2):
                    act.wait_ge(hu_ready, 2 * i + u + 1)
                    nc.scalar.copy(huh[:, u, :], hu[:, u, :]).then_inc(huh_ready, 1)

        @block.vector
        def _(dve):
            own = nc.vector
            dve.wait_ge(ld_tab, 16)
            dve.wait_ge(ld_filt, 16)
            own.tensor_copy(identh[:], ident).then_inc(ident_ready, 1)
            own.tensor_scalar(filt[:], filt[:], 1.0 / P, None, ALU.mult)
            dve.drain()
            own.tensor_scalar(fneg[:], filt[:, 1:6:2], -1.0, None, ALU.mult)
            for q in range(3):
                own.tensor_scalar(fa[:, q, :], cos_t, filt[:, 2 * q:2 * q + 1], None, ALU.mult)
                own.tensor_scalar(fb[:, q, :], sin_t, filt[:, 2 * q:2 * q + 1], None, ALU.mult)
            dve.drain()
            for q in range(3):
                own.scalar_tensor_tensor(fa[:, q, :], sin_t, fneg[:, q:q + 1], fa[:, q, :], ALU.mult, ALU.add)
                own.scalar_tensor_tensor(fb[:, q, :], cos_t, filt[:, 2 * q + 1:2 * q + 2], fb[:, q, :],
                                         ALU.mult, ALU.add)
            dve.drain().then_inc(filt_ready, 1)
            dve.wait_ge(filt_mm, 1)
            own.tensor_copy(cqk[:].rearrange("p a c -> p (a c)"), ps[:, 6, 0:2 * P]).then_inc(filt_cp, 1)
            own.tensor_copy(cv32[:], ps[:, 6, 2 * P:3 * P])
            dve.wait_ge(filt_mm, 2)
            own.tensor_copy(g32[:], ps[:, 7, 0:P])
            dve.drain()
            dve.wait_ge(pool_c, 1)
            own.reduce_max(mx_part[:, C_G:C_G + 1], g32[:], AX, apply_absolute_value=True)
            own.reduce_max(mx_part[:, C_V:C_V + 1], cv32[:], AX, apply_absolute_value=True)
            dve.wait_ge(ld_w, 5 * 16)
            own.reduce_max(mx_part[:, C_R:C_R + 1], wr_sb[:], AX, apply_absolute_value=True)
            own.reduce_max(mx_part[:, C_1:C_1 + 1], w1_sb[:], AX, apply_absolute_value=True)
            own.reduce_max(mx_part[:, C_2:C_2 + 1], w2_sb[:], AX, apply_absolute_value=True)
            own.reduce_max(mx_part[:, C_B:C_B + 1], b1_sb[:], AX, apply_absolute_value=True)
            dve.drain().then_inc(mx_ready, 1)
            dve.wait_ge(mx_red, 1)
            own.tensor_scalar(mx_all[:, 0:C_2], mx_all[:, 0:C_2], float(P), None, ALU.mult)
            dve.drain()
            own.tensor_tensor(mx_all[:, C_1:C_1 + 1], mx_all[:, C_1:C_1 + 1], mx_all[:, C_B:C_B + 1], ALU.max)
            dve.drain()
            own.tensor_scalar(mx_all[:], mx_all[:], 2.0 ** -90, None, ALU.max)
            dve.drain()
            bits = mx_all[:].bitcast(I32)
            own.tensor_scalar(bits, bits, 0x7F800000, None, ALU.bitwise_and)
            dve.drain()
            own.tensor_scalar(sc2[:].bitcast(I32), bits, -1.0, float((254 + 14) << 23), ALU.mult, ALU.add)
            dve.drain()
            own.reciprocal(inv2[:], sc2[:])
            dve.drain()
            own.tensor_scalar(inv_s[:], inv2[:, C_G:C_G + 1], float(1.0 / np.sqrt(P).astype(np.float32)), None, ALU.mult)
            own.tensor_tensor(inv12[:], inv2[:, C_1:C_1 + 1], inv2[:, C_2:C_2 + 1], ALU.mult)
            for hi, lo, full, c in ((gh, gl, g32, C_G), (cvh, cvl, cv32, C_V), (wrh, wrl, wr_sb, C_R),
                                    (w1h, w1l, w1_sb, C_1), (w2h, w2l, w2_sb, C_2)):
                own.tensor_scalar(hi[:], full[:], sc2[:, c:c + 1], None, ALU.mult)
                dve.drain()
                own.scalar_tensor_tensor(lo[:], full[:], sc2[:, c:c + 1], hi[:], ALU.mult, ALU.subtract)
            own.tensor_scalar(nb1[:], b1_sb[:], sc2[:, C_1:C_1 + 1], -1.0, ALU.mult, ALU.mult)
            dve.drain().then_inc(splits_ready, 1)
            dve.wait_ge(c_mm, 1)
            own.tensor_tensor(crow[:], ps[0:1, 6:8, :].rearrange("p b c -> p (b c)"), b2_sb[:], ALU.add)\
               .then_inc(c_row, 1)
            dve.wait_ge(c_bc, 1)
            own.tensor_copy(cbc[:], banks(6, E * P)).then_inc(c_ready, 1)

            for b in range(B):
                dve.wait_ge(z_ready, b + 1)
                for i in range(T):
                    own.bn_stats(bst[:, i, :], h[:, b * T + i, :])
                dve.drain()
                for i in range(T):
                    own.bn_aggr(zmv[:, b * T + i, :], bst[:, i, :])
                dve.drain().then_inc(zst_ready, 1)
            mean, var = zmv[:, :, 0], zmv[:, :, 1]
            own.tensor_tensor(tmp[:, 0, :], mean, mean, ALU.mult)
            dve.drain()
            own.tensor_tensor(tmp[:, 0, :], tmp[:, 0, :], var, ALU.add)
            dve.wait_ge(f_tanh, 1)
            own.tensor_tensor(tmp[:, 3, 0:1], th[:], th[:], ALU.mult)
            dve.drain()
            own.tensor_scalar(tmp[:, 0, :], tmp[:, 0, :], tmp[:, 3, 0:1], float(P), ALU.mult, ALU.mult)
            dve.drain().then_inc(f_pow, 1)
            dve.wait_ge(f_pow_done, 1)
            own.tensor_copy(f[:], tmp[:, 1, :])
            dve.drain()
            own.tensor_scalar(tmp[:, 1, :], tmp[:, 1, :], MIN_NORM, None, ALU.max)
            dve.drain().then_inc(f_tanh, 1)
            own.reciprocal(tmp[:, 3, :], tmp[:, 1, :])
            dve.wait_ge(f_tanh, 3)
            dve.drain()
            own.tensor_tensor(tmp[:, 2, :], tmp[:, 2, :], tmp[:, 3, :], ALU.mult)
            dve.drain()
            own.tensor_tensor(f[:], f[:], tmp[:, 2, :], ALU.mult)
            dve.drain()
            own.tensor_scalar(f[:], f[:], MIN_NORM, None, ALU.max)
            dve.drain()
            own.reciprocal(f[:], f[:])
            dve.drain()
            own.tensor_scalar(f[:], f[:], MAX_NORM, 1.0, ALU.mult, ALU.min)
            dve.drain()
            own.scalar_tensor_tensor(f[:], f[:], th[:], tmp[:, 2, :], ALU.mult, ALU.mult)
            dve.drain()
            own.tensor_tensor(tmp[:, 0, :], f[:], f[:], ALU.mult)
            dve.drain()
            own.tensor_tensor(tmp[:, 0, :], tmp[:, 0, :], var, ALU.mult)
            dve.drain()
            own.tensor_scalar(tmp[:, 0, :], tmp[:, 0, :], EPS_LN, None, ALU.add)
            dve.drain().then_inc(f_pow, 1)
            dve.wait_ge(f_pow_done, 2)
            own.tensor_tensor(frs[:], f[:], tmp[:, 1, :], ALU.mult)
            dve.drain()
            for b in range(B):
                cols = slice(b * NP, (b + 1) * NP)
                if b:
                    dve.wait_ge(xT_mm, b)
                for i in range(T):
                    t = b * T + i
                    own.tensor_scalar(xn[:, i, :], h[:, t, :], zmv[:, t, 0:1], frs[:, t:t + 1],
                                      ALU.subtract, ALU.mult)
                dve.drain().then_inc(xn_ready, 1)
                for i in range(T):
                    t = b * T + i
                    own.tensor_scalar(h[:, t, :], h[:, t, :], f[:, t:t + 1], None, ALU.mult)
                dve.wait_ge(xTh_ready, b + 1)
                own.tensor_tensor(xTl[:, cols], banks(4, NP), xTh[:, cols], ALU.subtract).then_inc(xTl_ready, 1)
                dve.wait_ge(yh_ready, b + 1)
                own.tensor_tensor(yTl[:, cols].rearrange("p (k c) -> p k c", k=2), ps[:, 6:8, 0:NP // 2],
                                  yTh[:, cols].rearrange("p (k c) -> p k c", k=2), ALU.subtract)\
                   .then_inc(yl_ready, 1)
            for t in range(B * T):
                u = t % 2
                dve.wait_ge(s_mm, t + 1)
                own.tensor_reduce(nmax[:, u:u + 1], ps[:, 2 * u:2 * u + 2, 0:KH],
                                  mybir.AxisListType.XY, ALU.max)
                dve.drain()
                own.tensor_scalar(nbias[:, u:u + 1], nmax[:, u:u + 1], inv_s[:], -1.0, ALU.mult, ALU.mult)\
                   .then_inc(nb_ready, 1)
                dve.wait_ge(pT_mm, t + 1)
                if t >= 1:
                    dve.wait_ge(o_mm, t)
                own.tensor_copy(probT[:, 512:NP], ps[:, 5, 0:NP - 512]).then_inc(pTb_ready, 1)
                own.reciprocal(rinv[:, u:u + 1], rsum[:, u:u + 1])
                dve.drain()
                dve.wait_ge(o_mm, t + 1)
                own.scalar_tensor_tensor(h[:, t, :], ps[:, 6 + u, 0:P], rinv[:, u:u + 1], h[:, t, :],
                                         ALU.mult, ALU.add).then_inc(o_used, 1)
                dve.drain()
                own.bn_stats(st6[:, u, :], h[:, t, :])
                dve.drain()
                own.bn_aggr(h2mv[:, t, :], st6[:, u, :])
            dve.drain()
            own.tensor_scalar(tmp[:, 0, :], h2mv[:, :, 1], EPS_LN, None, ALU.add)
            dve.drain().then_inc(rs2_in, 1)
            dve.wait_ge(rs2_ready, 1)
            for b in range(B):
                cols = slice(b * NP, (b + 1) * NP)
                if b:
                    dve.wait_ge(x2T_mm, b)
                for i in range(T):
                    t = b * T + i
                    own.tensor_scalar(xn[:, i, :], h[:, t, :], h2mv[:, t, 0:1], tmp[:, 1, t:t + 1],
                                      ALU.subtract, ALU.mult)
                dve.drain().then_inc(x2_ready, 1)
                dve.wait_ge(x2h_ready, b + 1)
                own.tensor_tensor(x2l[:], xn[:].rearrange("p t d -> p (t d)"), x2h[:], ALU.subtract)\
                   .then_inc(x2l_ready, 1)
                dve.wait_ge(x2T_mm, b + 1)
                own.tensor_copy(x2Tl[:, cols], banks(1, NP // 2).bitcast(F16)).then_inc(x2T_ready, 1)
            dve.wait_ge(lg_ready, B)
            bc = lambda ap: ap.unsqueeze(2).broadcast_to([P, B * T, E])
            rev = rev8[:].unsqueeze(1).broadcast_to([P, B * T, E])
            own.reduce_max(r1[:, 0, :], lg[:], AX)
            dve.drain()
            own.tensor_tensor(eq[:], lg[:], bc(r1[:, 0, :]), ALU.is_equal)
            dve.drain()
            own.tensor_tensor(cand[:], eq[:], rev, ALU.mult)
            dve.drain()
            own.reduce_max(r1[:, 1, :], cand[:], AX)
            dve.drain()
            own.tensor_tensor(m1h[:], bc(r1[:, 1, :]), rev, ALU.is_equal)
            dve.drain()
            own.scalar_tensor_tensor(lg2[:], m1h[:], -BIG, lg[:], ALU.mult, ALU.add)
            dve.drain()
            own.reduce_max(r1[:, 2, :], lg2[:], AX)
            dve.drain()
            own.tensor_tensor(eq[:], lg2[:], bc(r1[:, 2, :]), ALU.is_equal)
            own.tensor_tensor(r1[:, 4, :], r1[:, 2, :], r1[:, 0, :], ALU.subtract)
            dve.drain().then_inc(d_ready, 1)
            own.tensor_tensor(cand[:], eq[:], rev, ALU.mult)
            dve.drain()
            own.reduce_max(r1[:, 3, :], cand[:], AX)
            dve.drain()
            own.tensor_tensor(m2h[:], bc(r1[:, 3, :]), rev, ALU.is_equal)
            dve.wait_ge(e_ready, 1)
            own.tensor_scalar(r1[:, 0, :], r1[:, 5, :], 1.0, None, ALU.add)
            dve.drain()
            own.reciprocal(r1[:, 1, :], r1[:, 0, :])
            dve.drain()
            own.tensor_tensor(r1[:, 2, :], r1[:, 5, :], r1[:, 1, :], ALU.mult)
            dve.drain()
            own.tensor_tensor(eq[:], m1h[:], bc(r1[:, 1, :]), ALU.mult)
            own.tensor_tensor(cand[:], m2h[:], bc(r1[:, 2, :]), ALU.mult)
            dve.drain()
            own.tensor_tensor(comb[:], eq[:], cand[:], ALU.add)
            dve.drain()
            with dve.Fori(0, E) as e:
                with dve.Fori(0, B * T // 2) as j:
                    n0 = e * (B * T) + 2 * j
                    for u in range(2):
                        dve.wait_ge(h_mm, n0 + u + 1)
                        dve.wait_ge(hul_ready, 0)
                        own.tensor_tensor(
                            hu[:, u, :].rearrange("p (c n) -> p c n", c=HC),
                            ps[:, u, :].rearrange("p (c n) -> p c n", c=HC),
                            nb1[:, bass.ds(e * HC, HC)].unsqueeze(2).broadcast_to([P, HC, P]),
                            ALU.max).then_inc(hu_ready, 1)
                        dve.wait_ge(huh_ready, n0 + u + 1)
                        own.tensor_tensor(hul[:, u, :], hu[:, u, :], huh[:, u, :], ALU.subtract)\
                           .then_inc(hul_ready, 1)
                        dve.wait_ge(y2_mm, n0 + u + 1)
                        own.scalar_tensor_tensor(yv[:, u, :], ps[:, 4 + u, 0:P], inv12[:],
                                                 cbc[:, bass.ds(e * P, P)], ALU.mult, ALU.add)\
                           .then_inc(yv_ready, 1)
                        dve.drain()
                        acc = h[:, bass.ds(2 * j + u, 1), :].rearrange("p a d -> p (a d)")
                        own.scalar_tensor_tensor(
                            acc, yv[:, u, :],
                            comb[:, bass.ds(2 * j + u, 1), bass.ds(e, 1)].rearrange("p a b -> p (a b)"),
                            acc, ALU.mult, ALU.add).then_inc(acc_done, 1)

        @block.tensor
        def _(pe):
            mm = nc.tensor.matmul

            def three(out_ap, lhs, rhs, skip=False):
                (lh, ll), (rh, rl) = lhs, rhs
                mm(out_ap, lh, rh, start=True, stop=False)
                mm(out_ap, lh, rl, start=False, stop=False)
                return mm(out_ap, ll, rh, start=False, stop=True)

            pe.wait_ge(filt_ready, 1)
            for q in range(2):
                mm(ps[:, 6, q * P:q * P + P], fa[:, q, :], cos_t, start=True, stop=False)
                mm(ps[:, 6, q * P:q * P + P], fb[:, q, :], sin_t, start=False, stop=True)
            mm(ps[:, 6, 2 * P:3 * P], cos_t, fa[:, 2, :], start=True, stop=False)
            mm(ps[:, 6, 2 * P:3 * P], sin_t, fb[:, 2, :], start=False, stop=True).then_inc(filt_mm, 1)
            pe.wait_ge(filt_cp, 1)
            mm(ps[:, 7, 0:P], cqk[:, 0, :], cqk[:, 1, :], start=True, stop=True).then_inc(filt_mm, 1)
            pe.wait_ge(ld_w, 80)
            pe.wait_ge(splits_ready, 1)
            for e in range(E):
                for c in range(HC):
                    k = e * HC + c
                    last = mm(ps[0:1, 6 + e // 4, (e % 4) * P:(e % 4 + 1) * P], b1_sb[:, k:k + 1],
                              w2_sb[:, k * P:(k + 1) * P], start=(c == 0), stop=(c == HC - 1))
            last.then_inc(c_mm, 1)
            pe.wait_ge(c_row, 1)
            for k in range(2):
                last = mm(ps[:, 6 + k, :], onesrow[:], crow[:, k * 512:(k + 1) * 512], start=True, stop=True)
            last.then_inc(c_bc, 1)
            pe.wait_ge(ld_wb, 32)
            for b in range(B):
                pe.wait_ge(ld_seg, 32 * (b + 1))
                if b:
                    pe.wait_ge(segT_ready, b)
                for i in range(T):
                    last = nc.tensor.transpose(banks(0, NP)[0:K, i * P:(i + 1) * P], seg[:, b % 2, i, :], ident)
                last.then_inc(segT_mm, 1)
                pe.wait_ge(segT_ready, b + 1)
                if b:
                    pe.wait_ge(z_ready, b)
                for i in range(T):
                    last = mm(banks(2, NP)[:, i * P:(i + 1) * P], segT[:, i * P:(i + 1) * P], wb_sb[:],
                              start=True, stop=True)
                last.then_inc(z_mm, 1)
            pe.wait_ge(c_ready, 1)
            for b in range(B):
                c0 = b * NP
                pe.wait_ge(xn_ready, b + 1)
                if b:
                    pe.wait_ge(xTl_ready, b)
                for i in range(T):
                    last = nc.tensor.transpose(banks(4, NP)[:, i * P:(i + 1) * P], xn[:, i, :], ident)
                last.then_inc(xT_mm, 1)
                pe.wait_ge(xTl_ready, b + 1)
                if b:
                    pe.wait_ge(yl_ready, b)
                for k in range(2):
                    cols = slice(c0 + k * (NP // 2), c0 + (k + 1) * (NP // 2))
                    last = three(ps[:, 6 + k, 0:NP // 2], (gh[:], gl[:]), (xTh[:, cols], xTl[:, cols]))
                last.then_inc(y_mm, 1)
                if b:
                    pe.wait_ge(v_ready, b)
                for i in range(T):
                    cols = slice(c0 + i * P, c0 + (i + 1) * P)
                    last = three(banks(0, NP)[:, i * P:(i + 1) * P], (xTh[:, cols], xTl[:, cols]),
                                 (cvh[:], cvl[:]))
                last.then_inc(v_mm, 1)
            pe.wait_ge(yl_ready, B)
            pe.wait_ge(v_ready, B)

            def scores(t):
                b, u = t // T, t % 2
                q = slice(t * P, (t + 1) * P)
                for k in range(2):
                    keys = slice(b * NP + k * KH, b * NP + (k + 1) * KH)
                    last = three(ps[:, 2 * u + k, 0:KH], (yTh[:, q], yTl[:, q]), (xTh[:, keys], xTl[:, keys]))
                last.then_inc(s_mm, 1)

            scores(0)
            scores(1)
            for t in range(B * T):
                b, u = t // T, t % 2
                pe.wait_ge(p_ready, t + 1)
                if t >= 1:
                    pe.wait_ge(pTa_ready, t)
                    pe.wait_ge(pTb_ready, t)
                for i in range(T):
                    last = nc.tensor.transpose(banks(4, NP)[:, i * P:(i + 1) * P],
                                               prob[:, u, i * P:(i + 1) * P], ident)
                last.then_inc(pT_mm, 1)
                if t + 2 < B * T:
                    scores(t + 2)
                if t >= 2:
                    pe.wait_ge(o_used, t - 1)
                pe.wait_ge(pTa_ready, t + 1)
                pe.wait_ge(pTb_ready, t + 1)
                for i in range(T):
                    last = mm(ps[:, 6 + u, 0:P], probT[:, i * P:(i + 1) * P], v32[:, b * T + i, :],
                              start=(i == 0), stop=(i == T - 1))
                last.then_inc(o_mm, 1)
            for b in range(B):
                pe.wait_ge(x2l_ready, b + 1)
                if b:
                    pe.wait_ge(x2T_ready, 2 * b)
                for i in range(T):
                    nc.tensor.transpose(banks(0, NP // 2).bitcast(F16)[:, i * P:(i + 1) * P],
                                        x2h[:, i * P:(i + 1) * P], identh[:])
                    last = nc.tensor.transpose(banks(1, NP // 2).bitcast(F16)[:, i * P:(i + 1) * P],
                                               x2l[:, i * P:(i + 1) * P], identh[:])
                last.then_inc(x2T_mm, 1)
                pe.wait_ge(x2T_ready, 2 * b + 2)
                if b:
                    pe.wait_ge(lg_ready, b)
                for i in range(T):
                    cols = slice(b * NP + i * P, b * NP + (i + 1) * P)
                    last = three(ps[:, 2, i * E:(i + 1) * E], (x2Th[:, cols], x2Tl[:, cols]), (wrh[:], wrl[:]))
                last.then_inc(lg_mm, 1)

            def up(e, j, u, n):
                cols = bass.ds((2 * j + u) * P, P)
                for c in range(HC):
                    w = bass.ds(e * H + c * P, P)
                    last = three(ps[:, u, c * P:(c + 1) * P], (w1h[:, w], w1l[:, w]), (x2Th[:, cols], x2Tl[:, cols]))
                last.then_inc(h_mm, 1)

            with pe.Fori(0, E) as e:
                with pe.Fori(0, B * T // 2) as j:
                    n0 = e * (B * T) + 2 * j
                    for u in range(2):
                        up(e, j, u, n0)
                    for u in range(2):
                        pe.wait_ge(huh_ready, n0 + u + 1)
                        pe.wait_ge(hul_ready, n0 + u + 1)
                        for c in range(HC):
                            w = bass.ds(e * H + c * P, P)
                            hid = slice(c * P, (c + 1) * P)
                            mm(ps[:, 4 + u, 0:P], huh[:, u, hid], w2h[:, w], start=(c == 0), stop=False)
                            mm(ps[:, 4 + u, 0:P], huh[:, u, hid], w2l[:, w], start=False, stop=False)
                            last = mm(ps[:, 4 + u, 0:P], hul[:, u, hid], w2h[:, w], start=False,
                                      stop=(c == HC - 1))
                        last.then_inc(y2_mm, 1)
                    pe.wait_ge(yv_ready, n0 + 2)


def _tables():
    k = np.arange(P)
    a = 2 * np.pi * ((k[:, None] * k[None, :]) % P) / P
    tri = (k[:, None] < k[None, :]).astype(np.float64)
    return np.concatenate([np.cos(a), np.sin(a), np.eye(P), tri], 1).astype(np.float32)


def kernel(**inputs):
    import concourse.bacc as bacc
    from concourse.bass_utils import run_bass_kernel_spmd

    a = {k: np.ascontiguousarray(v) for k, v in inputs.items()}
    ins = {
        "x": a["x"],
        "wb": np.concatenate([a["L0_tok_W"], a["L0_tok_b"][None]], 0),
        "scale": np.repeat(a["L0_tok_effective_scale"][None], P, 0),
        "tables": _tables(),
        "filters": np.stack([a["L0_attn_" + n] for n in ("q_real", "q_imag", "k_real", "k_imag", "v_real", "v_imag")], 1),
        "wr": a["L0_ffn_W_router"],
        "w1": np.ascontiguousarray(a["L0_ffn_W1"].transpose(1, 0, 2).reshape(P, E * H)),
        "b1t": np.ascontiguousarray(a["L0_ffn_b1"].reshape(E * HC, P).T),
        "w2": np.ascontiguousarray(a["L0_ffn_W2"].reshape(E * HC, P, P).transpose(1, 0, 2).reshape(P, E * H)),
        "b2": a["L0_ffn_b2"].reshape(1, E * P),
    }
    ins = {k: np.ascontiguousarray(v) for k, v in ins.items()}
    nc = bacc.Bacc("TRN2", target_bir_lowering=False, num_devices=1)
    aps = [nc.dram_tensor("in_" + k, v.shape, F32, kind="ExternalInput").ap() for k, v in ins.items()]
    out = nc.dram_tensor("out", (B, N, P), F32, kind="ExternalOutput").ap()
    build(nc, *aps, out)
    r = run_bass_kernel_spmd(nc, [{"in_" + k: v for k, v in ins.items()}], core_ids=[0])
    return r.results[0]["out"]
```

```python
from contextlib import ExitStack

import numpy as np

import concourse.bass as bass
from concourse import mybir

F32 = mybir.dt.float32
F16 = mybir.dt.float16
BF16 = mybir.dt.bfloat16
I32 = mybir.dt.int32
U32 = mybir.dt.uint32
ALU = mybir.AluOpType
ACT = mybir.ActivationFunctionType
AX = mybir.AxisListType.X

P = 128
B, L = 4, 20000
SEG, STRIDE = 48, 24
N = (L - SEG) // STRIDE + 1
T = -(-N // P)
LAST = N - (T - 1) * P
NP = T * P
KH = N // 2
NT = B * T
E, H = 8, 512
HC = H // P
K = SEG + 1
EPS_LN = 1e-5
MIN_NORM = 1e-15
MAX_NORM = 1.0 - 0.004
S = 2 * P
R = B * N + S
DUMMY = E * R
ROW = P + 2
NS = (2 * B * N + E * (S - 1)) // S
RING = 4
ACT_TILES = 3
PACK = 8
NOWHERE = 16384.0
WC = 512
NCH = 2 * E
GROUPS = ((0, 4), (4, 7), (7, 11), (11, 14), (14, 17), (17, 19), (19, 21), (21, 23), (23, 25), (25, 28))
NGR = len(GROUPS)
W_MAX, W_SCALE, W_SPLIT0 = 9, 10, 11

def build(nc, x, wb, scale1, tables, filters, wr, w1, b1t, w2, b2, out):
    ctx = ExitStack()
    with ctx:
        def sb(name, shape, dt=F32):
            return ctx.enter_context(nc.sbuf_tensor(name, shape, dt))

        def sem(name):
            return ctx.enter_context(nc.semaphore(name))

        ps = ctx.enter_context(nc.psum_tensor("ps", [P, 8, 512], F32))

        def banks(b, cols):
            return ps[:, b:b + -(-cols // 512), :].rearrange("p b c -> p (b c)")[:, 0:cols]

        tab = sb("tab", [P, 4 * P])
        cos_t, sin_t, ident = tab[:, 0:P], tab[:, P:2 * P], tab[:, 2 * P:3 * P]
        identh, trib, ones = sb("identh", [P, P], F16), sb("trib", [P, P], BF16), sb("ones", [P, P], BF16)
        filt = sb("filt", [P, 6])
        wb_sb = sb("wb_sb", [K, P])
        sc_in = sb("sc_in", [P, 1])
        wr_sb = sb("wr_sb", [P, E])
        b1_sb = sb("b1_sb", [P, E * HC])
        b2_sb = sb("b2_sb", [P, E])
        wall = sb("wall", [P, NCH + 2, WC])
        raw = [wall[:, k + 2, :] for k in range(NCH)]
        wall16 = wall[:].rearrange("p k c -> p (k c)").bitcast(F16)
        w_hi = [wall16[:, 2 * WC * k:2 * WC * k + WC] for k in range(NCH)]
        w_lo = [wall16[:, 2 * WC * k + WC:2 * WC * (k + 1)] for k in range(NCH)]
        fa = sb("fa", [P, 3, P])
        fb = sb("fb", [P, 3, P])
        fneg = sb("fneg", [P, 3])
        cqk = sb("cqk", [P, 2, P])
        g32 = sb("g32", [P, P])
        cv32 = sb("cv32", [P, P])
        gh, gl = sb("gh", [P, P], F16), sb("gl", [P, P], F16)
        cvh, cvl = sb("cvh", [P, P], F16), sb("cvl", [P, P], F16)
        wrh, wrl = sb("wrh", [P, E], F16), sb("wrl", [P, E], F16)
        nb1 = sb("nb1", [P, E * HC])
        nb1h, nb1l = sb("nb1h", [P, E * HC], F16), sb("nb1l", [P, E * HC], F16)
        mx_w = sb("mx_w", [P, NCH])
        mx_part, mx_all = sb("mx_part", [P, 6]), sb("mx_all", [P, 6])
        sc2, inv2 = sb("sc2", [P, 6]), sb("inv2", [P, 6])
        inv_s, inv12, sc12 = sb("inv_s", [P, 1]), sb("inv12", [P, 1]), sb("sc12", [P, 1])
        cc = sb("cc", [P, E])
        cbf, c24 = sb("cbf", [P, 3, E], BF16), sb("c24", [P, 3, E])
        c3 = sb("c3", [P, P], BF16)
        own_rows = sb("own_rows", [P, E])
        pick = sb("pick", [P, E, P], BF16)

        seg = sb("seg", [P, B, T, K])
        segT = sb("segT", [K, 2, NP])
        h = sb("h", [P, NT, P])
        zmv = sb("zmv", [P, NT, 2])
        bst = sb("bst", [P, T, 6])
        f, frs, nmf = (sb(n, [P, NT]) for n in ("f", "frs", "nmf"))
        tmp = sb("tmp", [P, 5, NT])
        half_c, mhalf_c = sb("half_c", [P, NT]), sb("mhalf_c", [P, NT])
        th = sb("th", [P, 2])
        xn = sb("xn", [P, T, P])
        xTh, xTl = sb("xTh", [P, B * NP], F16), sb("xTl", [P, B * NP], F16)
        yTh, yTl = sb("yTh", [P, B * NP], F16), sb("yTl", [P, B * NP], F16)
        v32 = sb("v32", [P, NT, P])
        prob = sb("prob", [P, 2, NP])
        probT = sb("probT", [P, 2, NP])
        nmax, nbias, rsum, rinv = (sb(n, [P, 2]) for n in ("nmax", "nbias", "rsum", "rinv"))
        st6 = sb("st6", [P, 2, 6])
        h2mv = sb("h2mv", [P, NT, 2])
        veps, rstd = sb("veps", [P, NT]), sb("rstd", [P, NT])
        x2f = sb("x2f", [P, 2, P])
        rowA, rowB = sb("rowA", [P, NT, ROW]), sb("rowB", [P, NT, ROW])
        rows = (rowA, rowB)

        def halves(row):
            return row[:, :, 0:P].bitcast(F16)

        x2T = sb("x2T", [P, 2, 2 * P], F16)
        lg, top8 = sb("lg", [P, NT, E]), sb("top8", [P, NT, E])
        ix8 = sb("ix8", [P, NT, E], U32)
        ixf = sb("ixf", [P, NT, 2])
        gate = sb("gate", [P, 3, NT])
        GN = max(z - a for a, z in GROUPS)
        m12 = sb("m12", [P, 2, NT, E])
        mh = sb("mh", [P, NT, E], BF16)
        hist = sb("hist", [P, NGR, E])
        seen = sb("seen", [P, NGR + 1, E], BF16)
        posb = sb("posb", [P, GN, E])
        q12 = sb("q12", [P, 2, GN, E])
        nowhere = sb("nowhere", [P, 1], I32)
        slotf = sb("slotf", [P, 2, GN])
        slot = sb("slot", [P, 2, NT], I32)
        iota8, ebase = sb("iota8", [P, E]), sb("ebase", [P, E])
        stepno = sb("stepno", [P, NS])
        ntl, cum, one8 = (sb(n, [P, E]) for n in ("ntl", "cum", "one8"))
        cnti, ntli = sb("cnti", [P, E], I32), sb("ntli", [P, E], I32)
        past, pastn = sb("past", [P, NS, E]), sb("pastn", [P, NS, E])
        ej, sj = sb("ej", [P, NS]), sb("sj", [P, NS])
        onehot = sb("onehot", [P, NS, E])
        nbp, nbs = sb("nbp", [P, NS, HC, E]), sb("nbs", [P, NS + 2, HC])
        step_e = sb("step_e", [P, NS + 1])
        tab_e = sb("tab_e", [P, NS + 1], I32)
        pow8, packed = sb("pow8", [P, PACK]), sb("packed", [P, (NS - 1) // PACK, PACK])
        packf, tab_pack = sb("packf", [P, (NS - 1) // PACK]), sb("tab_pack", [P, (NS - 1) // PACK], I32)
        tab_row = sb("tab_row", [P, NS], I32)
        tab_pad = sb("tab_pad", [P, E], I32)
        pad_row = sb("pad_row", [P, 2, ROW])
        xin = sb("xin", [P, RING, 2, ROW])
        ixy = sb("ixy", [P, RING, 2], I32)
        wy = sb("wy", [P, RING, 2])
        xeT = sb("xeT", [P, 2, 2 * S], F16)
        yb = sb("yb", [P, RING, 2, P])
        hu = v32[:].rearrange("p t d -> p (t d)")[:, 0:2 * HC * S].rearrange("p (u c) -> p u c", u=2)
        huh = xTh[:, 0:2 * HC * S].rearrange("p (u c) -> p u c", u=2)
        hul = xTl[:, 0:2 * HC * S].rearrange("p (u c) -> p u c", u=2)
        yin = [buf.rearrange("p (t k d) -> p t k d", t=T, k=2) for buf in (
            prob[:].rearrange("p a c -> p (a c)"), probT[:].rearrange("p a c -> p (a c)"),
            yTh[:].bitcast(F32), yTl[:].bitcast(F32))]

        xbuf = nc.dram_tensor("xbuf", [DUMMY + S, ROW], F32, kind="Internal").ap()
        ybuf = nc.dram_tensor("ybuf", [2 * B * N, P], F32, kind="Internal").ap()

        (ld_tab, ld_wb, ld_filt, ld_small, ld_w1, ld_w2, st_out) = map(sem, (
            "ld_tab", "ld_wb", "ld_filt", "ld_small", "ld_w1", "ld_w2", "st_out"))
        ld_seg = [sem(f"ld_seg{b}") for b in range(B)]
        (filt_ready, filt_mm, filt_cp, mx_ready, mx_red, splits_ready, ident_ready, c_mm, c24_ready, c3_mm,
         pick_ready, pool_c, ones_seg, pad_const, w_scaled, wh_ready, wl_ready) = map(sem, (
             "filt_ready", "filt_mm", "filt_cp", "mx_ready", "mx_red", "splits_ready", "ident_ready",
             "c_mm", "c24_ready", "c3_mm", "pick_ready", "pool_c", "ones_seg", "pad_const", "w_scaled",
             "wh_ready", "wl_ready"))
        (segT_mm, segT_ready, z_mm, z_ready, scale_ready, sq_in, sq_ready, clamp_ready, tanh_ready, var1_ready,
         inv1_ready, nmf_ready, xa_ready, xn_ready, h_ready, xT_mm, xTh_ready, xTl_ready, y_mm, yh_ready, yl_ready,
         v_mm, v_ready) = map(sem, (
             "segT_mm", "segT_ready", "z_mm", "z_ready", "scale_ready", "sq_in", "sq_ready", "clamp_ready",
             "tanh_ready", "var1_ready", "inv1_ready", "nmf_ready", "xa_ready", "xn_ready", "h_ready", "xT_mm",
             "xTh_ready", "xTl_ready", "y_mm", "yh_ready", "yl_ready", "v_mm", "v_ready"))
        (s_mm, nb_ready, p_ready, pT_mm, pT_ready, o_mm, o_used) = map(sem, (
            "s_mm", "nb_ready", "p_ready", "pT_mm", "pT_ready", "o_mm", "o_used"))
        (var_ready, rstd_ready, x2_ready, x2h_ready, x2l_ready, x2T_mm, x2T_ready, lg_mm, lg_ready,
         d_ready, e_ready, m_ready, pos_mm, pos_used, slot_ready, cnt_mm, cnt_ready, table_ready, c3_ready,
         pads_stored, dispatched) = map(sem, (
             "var_ready", "rstd_ready", "x2_ready", "x2h_ready", "x2l_ready", "x2T_mm", "x2T_ready",
             "lg_mm", "lg_ready", "d_ready", "e_ready", "m_ready", "pos_mm", "pos_used", "slot_ready",
             "cnt_mm", "cnt_ready", "table_ready", "c3_ready", "pads_stored", "dispatched"))
        dup_ready = [sem(f"dup_ready{g}") for g in range(NGR)]
        xin_ready = [sem(f"xin_ready{r}") for r in range(RING)]
        (ix_ready, wy_ready, xe_mm, xe_ready, h_mm, hu_ready, huh_ready, hul_ready, e_mm,
         y_ready, y_seen, out_ready) = map(sem, (
             "ix_ready", "wy_ready", "xe_mm", "xe_ready", "h_mm", "hu_ready",
             "huh_ready", "hul_ready", "e_mm", "y_ready", "y_seen", "out_ready"))
        yin_ready = [sem(f"yin_ready{b}") for b in range(B)]
        yb_free = [sem(f"yb_free{r}") for r in range(RING)]

        C_G, C_V, C_R, C_1, C_2, C_B = range(6)
        TAIL = 6

        def route_steps(t):
            first = [g for g, (_, z) in enumerate(GROUPS) if z + TAIL == t]
            second = [g for g, (_, z) in enumerate(GROUPS) if z + TAIL + 1 == t]
            return first, second

        NSTEP = NT + TAIL + 2

        SETS = ((0, 1), (1, 2), (2, B))

        def cols_of(q):
            return slice(SETS[q][0] * T, SETS[q][1] * T)

        def store_pad(eng, row0):
            eng.dma_start(xbuf[row0, :].rearrange("(p j) d -> p j d", j=2), pad_row[:]).then_inc(pads_stored, 16)

        block = ctx.enter_context(nc.Block())

        @block.sync
        def _(sp):
            for b in range(B):
                sp.dma_start(seg[:, b, 0:T - 1, 0:SEG],
                             bass.AP(tensor=x.tensor, offset=b * L,
                                     ap=[[STRIDE, P], [STRIDE * P, T - 1], [1, SEG]])).then_inc(ld_seg[b], 16)
                if b == 0:
                    sp.wait_ge(ones_seg, 1)
                sp.dma_start(seg[0:LAST, b, T - 1, 0:SEG],
                             bass.AP(tensor=x.tensor, offset=b * L + STRIDE * P * (T - 1),
                                     ap=[[STRIDE, LAST], [1, SEG]])).then_inc(ld_seg[b], 16)
            for dst, src in ((wr_sb, wr), (b1_sb, b1t), (b2_sb, b2)):
                sp.dma_start(dst[:], src).then_inc(ld_small, 16)
            sp.dma_start(wall[:, 2 + E:2 + 2 * E, :], w2.rearrange("p (k c) -> p k c", c=WC)).then_inc(ld_w2, 16)
            sp.dma_start(wall[:, 2:2 + E, :], w1.rearrange("p (k c) -> p k c", c=WC)).then_inc(ld_w1, 16)

            sp.wait_ge(pad_const, 1)
            store_pad(sp, slice(DUMMY, DUMMY + S))
            for g, (a, z) in enumerate(GROUPS):
                sp.wait_ge(x2l_ready, z)
                sp.dma_start(rowB[:, a:z, 0:P], rowA[:, a:z, 0:P]).then_inc(dup_ready[g], 16)
            sp.wait_ge(cnt_ready, 1)
            for e in range(E // 2):
                row = sp.value_load(tab_pad[0:1, e:e + 1], min_val=0, max_val=DUMMY - S)
                store_pad(sp, bass.ds(row, S))

            def load_rows(i, u, row0):
                n = RING * i + u
                sp.wait_ge(xe_mm, n + 1)
                sp.wait_ge(ix_ready, n + 1)
                sp.wait_ge(wy_ready, n + 1)
                sp.dma_start(xin[:, u % RING, :, :],
                             xbuf[row0, :].rearrange("(p j) d -> p j d", j=2)).then_inc(xin_ready[u % RING], 16)

            def row_of(n):
                return bass.ds(sp.value_load(tab_row[0:1, n], min_val=0, max_val=DUMMY), S)

            sp.wait_ge(table_ready, 1)
            row0 = row_of(slice(0, 1))
            sp.wait_ge(pads_stored, 16 * (E + 1))
            sp.wait_ge(dispatched, 16 * 2 * NT)
            load_rows(0, 0, row0)
            with sp.Fori(0, (NS - 1) // RING) as i:
                for u in range(1, RING + 1):
                    load_rows(i, u, row_of(bass.ds(RING * i + u, 1)))
            for n in range(NS, NS + 2):
                load_rows(0, n, slice(DUMMY, DUMMY + S))

            def load_results(b):
                src = ybuf[2 * N * b:2 * N * (b + 1), :].rearrange("(n k) d -> n (k d)", k=2)
                dst = yin[b].rearrange("p i k d -> p i (k d)")
                sp.dma_start(dst[:, 0:T - 1, :], src[0:N - LAST, :].rearrange("(i p) d -> p i d", p=P))\
                    .then_inc(yin_ready[b], 16)
                sp.dma_start(dst[0:LAST, T - 1, :], src[N - LAST:N, :]).then_inc(yin_ready[b], 16)

            for r in range(RING):
                sp.wait_ge(yb_free[r], 16 + 32 * len(range(r, NS, RING)))
            for b in range(B):
                load_results(b)
            for b in range(B):
                sp.wait_ge(out_ready, b + 1)
                sp.dma_start(out[b, 0:N - LAST, :].rearrange("(i p) d -> p i d", p=P),
                             h[:, b * T:b * T + T - 1, :]).then_inc(st_out, 16)
                sp.dma_start(out[b, N - LAST:N, :], h[0:LAST, b * T + T - 1, :]).then_inc(st_out, 16)
            sp.wait_ge(st_out, 32 * B)

        @block.gpsimd
        def _(pool):
            pool.memset(seg[:, :, T - 1, :], 0.0)
            pool.memset(mx_part[:], 0.0)
            pool.drain()
            pool.memset(seg[:, :, :, SEG:K], 1.0).then_inc(ones_seg, 1)
            pool.memset(half_c[:], 0.5)
            pool.memset(mhalf_c[:], -0.5)
            pool.drain().then_inc(pool_c, 1)

            def norm(q):
                c = cols_of(q)
                pool.wait_ge(sq_in, q + 1)
                pool.tensor_tensor(tmp[:, 1, c], tmp[:, 0, c], half_c[:, c], ALU.pow).then_inc(sq_ready, 1)

            def inverse(q):
                c = cols_of(q)
                pool.wait_ge(var1_ready, q + 1)
                pool.tensor_tensor(tmp[:, 4, c], tmp[:, 3, c], mhalf_c[:, c], ALU.pow).then_inc(inv1_ready, 1)

            def embed(b):
                c = slice(b * T, (b + 1) * T)
                pool.wait_ge(xn_ready, b + 1)
                pool.wait_ge(xa_ready, ACT_TILES * (b + 1))
                pool.tensor_tensor(h[:, c, :], h[:, c, :], f[:, c].unsqueeze(2).broadcast_to([P, T, P]),
                                   ALU.mult).then_inc(h_ready, 1)

            norm(0)
            norm(1)
            inverse(0)
            pool.wait_ge(mx_ready, 1)
            pool.partition_all_reduce(mx_all[:, C_G:C_1], mx_part[:, C_G:C_1], P,
                                      bass.bass_isa.ReduceOp.max).then_inc(mx_red, 1)
            norm(2)
            inverse(1)
            inverse(2)
            for b in range(B):
                embed(b)
            pool.memset(prob[:, :, N:NP], 0.0)
            pool.memset(ones[:], 1.0)
            pool.memset(one8[:], 1.0)
            pool.memset(c3[:], 0.0)
            pool.memset(mh[:], 0.0)
            pool.memset(seen[:], 0.0)
            pool.memset(pad_row[:], 0.0)
            pool.memset(slot[:], 2 * DUMMY)
            pool.memset(step_e[:], 0.0)
            for k in range(PACK):
                pool.memset(pow8[:, k:k + 1], float(E ** k))
            pool.memset(nowhere[:], int(NOWHERE))
            pool.memset(nbs[:, NS:NS + 2, :], 0.0)
            exact = dict(allow_small_or_imprecise_dtypes=True)
            pool.iota(iota8[:], pattern=[[1, E]], base=0, channel_multiplier=0, **exact)
            pool.iota(ebase[:], pattern=[[R, E]], base=0, channel_multiplier=0, **exact)
            pool.iota(stepno[:], pattern=[[1, NS]], base=0, channel_multiplier=0, **exact)
            for b in range(B):
                for k in range(2):
                    pool.iota(rows[k][:, b * T:b * T + T, ROW - 1], pattern=[[2 * P, T]], base=2 * N * b + k,
                              channel_multiplier=2, **exact)
            pool.drain().then_inc(pool_c, 1)
            pool.memset(pad_row[:, :, ROW - 1], NOWHERE)
            pool.drain().then_inc(pad_const, 1)
            for free in (xe_mm, ix_ready, wy_ready):
                pool.sem_inc(free, RING)

            for r in range(RING):
                pool.indirect_dma_start(
                    ybuf, bass.IndirectOffsetOnAxis(ap=nowhere[:], axis=0), pad_row[:, 0, 0:P], None,
                    bounds_check=2 * B * N - 1, oob_is_err=False).then_inc(yb_free[r], 16)

            pool.tensor_tensor(own_rows[:], ident[:, 0:E], ident[:, E:2 * E], ALU.add)
            pool.drain()
            pool.tensor_tensor(own_rows[:], own_rows[:], ident[:, 2 * E:3 * E], ALU.add)
            pool.drain()
            pool.tensor_copy(pick[:], own_rows[:].unsqueeze(2).broadcast_to([P, E, P]))
            pool.drain().then_inc(pick_ready, 1)

            todo = [(g, t, k) for g, (a, z) in enumerate(GROUPS) for t in range(a, z) for k in range(2)]

            def dispatch():
                g, t, k = todo.pop(0)
                if (t, k) == (GROUPS[g][0], 0):
                    pool.wait_ge(slot_ready, g + 1)
                    pool.wait_ge(dup_ready[g], 16)
                v = LAST if t % T == T - 1 else P
                pool.indirect_dma_start(
                    xbuf, bass.IndirectOffsetOnAxis(ap=slot[0:v, k, t:t + 1], axis=0), rows[k][0:v, t, :], None,
                    bounds_check=DUMMY - 1, oob_is_err=False).then_inc(dispatched, 16)

            for t in range(NT):
                pool.wait_ge(var_ready, t + 1)
                pool.tensor_tensor(rstd[:, t:t + 1], veps[:, t:t + 1], mhalf_c[:, 0:1], ALU.pow)\
                    .then_inc(rstd_ready, 1)
                if t == W_MAX - 1:
                    pool.wait_ge(mx_ready, 2)
                    pool.partition_all_reduce(mx_all[:, C_1:], mx_part[:, C_1:], P,
                                              bass.bass_isa.ReduceOp.max).then_inc(mx_red, 1)
                for _ in range(3 if t < NT - 4 else 2):
                    if GROUPS[todo[0][0]][1] + TAIL + 1 <= t + 2:
                        dispatch()
            while todo:
                dispatch()

            def give_back(i, u):
                n = RING * i + u
                for j in range(2):
                    pool.wait_ge(y_ready, 2 * n + j + 1)
                    pool.sem_inc(y_seen, 1)
                    pool.indirect_dma_start(
                        ybuf, bass.IndirectOffsetOnAxis(ap=ixy[:, u % RING, j:j + 1], axis=0),
                        yb[:, u % RING, j, :], None,
                        bounds_check=2 * B * N - 1, oob_is_err=False).then_inc(yb_free[u % RING], 16)

            give_back(0, 0)
            with pool.Fori(0, (NS - 1) // RING) as i:
                for u in range(1, RING + 1):
                    give_back(i, u)

        @block.scalar
        def _(act):
            def seg_copy(b):
                act.wait_ge(segT_mm, b + 1)
                if b >= 2:
                    act.wait_ge(z_mm, b - 1)
                nc.scalar.copy(segT[:, b % 2, :], banks(4 * (b % 2), NP)[0:K, :]).then_inc(segT_ready, 1)

            def z_copy(b):
                act.wait_ge(z_mm, b + 1)
                nc.scalar.copy(h[:, b * T:b * T + T, :].rearrange("p t d -> p (t d)"),
                               banks(2, NP)).then_inc(z_ready, 1)

            def tanh_norm(q):
                act.wait_ge(clamp_ready, q + 1)
                nc.scalar.activation(tmp[:, 2, cols_of(q)], tmp[:, 4, cols_of(q)], ACT.Tanh)\
                    .then_inc(tanh_ready, 1)

            def shift_scale(b):
                act.wait_ge(nmf_ready, min(b, 2) + 1)
                if b:
                    act.wait_ge(xT_mm, b)
                for t in range(b * T, b * T + ACT_TILES):
                    nc.scalar.activation(xn[:, t - b * T, :], h[:, t, :], ACT.Identity, scale=frs[:, t:t + 1],
                                         bias=nmf[:, t:t + 1]).then_inc(xa_ready, 1)

            def x_high(b):
                act.wait_ge(xT_mm, b + 1)
                nc.scalar.copy(xTh[:, b * NP:(b + 1) * NP], banks(4, NP)).then_inc(xTh_ready, 1)

            def y_high(b):
                act.wait_ge(y_mm, b + 1)
                nc.scalar.copy(yTh[:, b * NP:(b + 1) * NP].rearrange("p (k c) -> p k c", k=2),
                               ps[:, 6:8, 0:NP // 2]).then_inc(yh_ready, 1)

            def values(b):
                act.wait_ge(v_mm, b + 1)
                nc.scalar.activation(v32[:, b * T:b * T + T, :].rearrange("p t d -> p (t d)"), banks(0, NP),
                                     ACT.Copy, scale=inv2[:, C_V:C_V + 1]).then_inc(v_ready, 1)

            act.dma_start(tab[:], tables).then_inc(ld_tab, 16)
            act.dma_start(filt[:], filters).then_inc(ld_filt, 16)
            act.dma_start(wb_sb[:], wb).then_inc(ld_wb, 16)
            act.dma_start(sc_in[:], scale1).then_inc(ld_wb, 16)
            seg_copy(0)
            act.wait_ge(ld_wb, 32)
            nc.scalar.activation(th[:, 0:1], sc_in[:], ACT.Tanh).then_inc(scale_ready, 1)
            seg_copy(1)
            z_copy(0)
            seg_copy(2)
            z_copy(1)
            seg_copy(3)
            tanh_norm(0)
            z_copy(2)
            z_copy(3)
            shift_scale(0)
            x_high(0)
            tanh_norm(1)
            shift_scale(1)
            tanh_norm(2)
            act.wait_ge(splits_ready, 1)
            for b in range(B):
                if b + 1 < B:
                    x_high(b + 1)
                if b + 2 < B:
                    shift_scale(b + 2)
                y_high(b)
                values(b)

            def softmax_exp(t):
                u = t % 2
                act.wait_ge(nb_ready, t + 1)
                if t >= 2:
                    act.wait_ge(pT_mm, t - 1)
                    act.wait_ge(o_used, t - 1)
                nc.scalar.activation(prob[:, u, 0:N].rearrange("p (k c) -> p k c", k=2),
                                     ps[:, 2 * u:2 * u + 2, 0:KH], ACT.Exp, bias=nbias[:, u:u + 1],
                                     scale=inv_s[:], accum_out=rsum[:, u:u + 1]).then_inc(p_ready, 1)

            softmax_exp(0)
            for t in range(NSTEP):
                m = t - 4
                if 0 <= m < NT:
                    act.wait_ge(x2_ready, m + 1)
                    nc.scalar.copy(halves(rowA)[:, m, 0:P], x2f[:, m % 2, :]).then_inc(x2h_ready, 1)
                m = t - 5
                if 0 <= m < NT:
                    act.wait_ge(x2T_mm, m + 1)
                    nc.scalar.copy(x2T[:, m % 2, :], ps[:, 7, 0:P].bitcast(F16)).then_inc(x2T_ready, 1)
                if t < NT:
                    act.wait_ge(pT_mm, t + 1)
                    if t >= 2:
                        act.wait_ge(o_mm, t - 1)
                    nc.scalar.copy(probT[:, t % 2, :], banks(4, NP)).then_inc(pT_ready, 1)
                if t + 1 < NT:
                    softmax_exp(t + 1)
                if 0 <= m < NT:
                    act.wait_ge(lg_mm, m + 1)
                    nc.scalar.copy(lg[:, m, :], ps[:, 5, NP - 512:NP - 512 + E]).then_inc(lg_ready, 1)
                for g in route_steps(t)[0]:
                    a, z = GROUPS[g]
                    act.wait_ge(d_ready, g + 1)
                    nc.scalar.activation(gate[:, 1, a:z], gate[:, 0, a:z], ACT.Exp,
                                         scale=inv2[:, C_R:C_R + 1]).then_inc(e_ready, 1)
                k = t - W_SPLIT0
                if 0 <= k < NCH:
                    if k == 0:
                        act.wait_ge(w_scaled, 1)
                    if k >= 2:
                        act.wait_ge(wl_ready, k - 1)
                    c = C_1 if k < E else C_2
                    nc.scalar.activation(w_hi[k], raw[k], ACT.Copy, scale=sc2[:, c:c + 1]).then_inc(wh_ready, 1)

            act.wait_ge(pad_const, 1)
            act.wait_ge(cnt_ready, 1)
            for e in range(E // 2, E):
                row = act.value_load(tab_pad[0:1, e:e + 1], min_val=0, max_val=DUMMY - S)
                store_pad(act, bass.ds(row, S))

            def take_rows(i, u):
                n = RING * i + u
                act.wait_ge(xe_mm, n + 1 + RING)
                nc.scalar.copy(xeT[:, u % 2, :], ps[:, 4 + u % 2, 0:S].bitcast(F16)).then_inc(xe_ready, 1)

            def high(i, u):
                n = RING * i + u
                for q in range(2):
                    act.wait_ge(hu_ready, 2 * n + q + 1)
                    nc.scalar.copy(huh[:, u % 2, q * 2 * S:(q + 1) * 2 * S],
                                   hu[:, u % 2, q * 2 * S:(q + 1) * 2 * S]).then_inc(huh_ready, 1)

            def weigh(i, u):
                n = RING * i + u
                act.wait_ge(e_mm, n + 1)
                act.wait_ge(wy_ready, n + 1 + RING)
                act.wait_ge(yb_free[u % RING], 32 * (i + u // RING) + 16)
                for j in range(2):
                    nc.scalar.activation(yb[:, u % RING, j, :], ps[:, 6 + u % 2, j * P:(j + 1) * P], ACT.Copy,
                                         scale=wy[:, u % RING, j:j + 1]).then_inc(y_ready, 1)

            take_rows(0, 0)
            take_rows(0, 1)
            high(0, 0)
            act.wait_ge(h_mm, 2)
            take_rows(0, 2)
            high(0, 1)
            weigh(0, 0)
            with act.Fori(0, (NS - 1) // RING) as i:
                for u in range(1, RING + 1):
                    take_rows(i, u + 2)
                    high(i, u + 1)
                    weigh(i, u)

        @block.vector
        def _(dve):
            own = nc.vector
            dve.wait_ge(pool_c, 1)
            dve.wait_ge(ld_tab, 16)
            dve.wait_ge(ld_filt, 16)
            own.tensor_scalar(filt[:], filt[:], 1.0 / P, None, ALU.mult)
            dve.drain()
            own.tensor_scalar(fneg[:], filt[:, 1:6:2], -1.0, None, ALU.mult)
            for q in range(3):
                own.tensor_scalar(fa[:, q, :], cos_t, filt[:, 2 * q:2 * q + 1], None, ALU.mult)
                own.tensor_scalar(fb[:, q, :], sin_t, filt[:, 2 * q:2 * q + 1], None, ALU.mult)
            dve.drain()
            for q in range(3):
                own.scalar_tensor_tensor(fa[:, q, :], sin_t, fneg[:, q:q + 1], fa[:, q, :], ALU.mult, ALU.add)
                own.scalar_tensor_tensor(fb[:, q, :], cos_t, filt[:, 2 * q + 1:2 * q + 2], fb[:, q, :],
                                         ALU.mult, ALU.add)
            dve.drain().then_inc(filt_ready, 1)
            own.tensor_copy(identh[:], ident)
            own.tensor_copy(trib[:], tab[:, 3 * P:4 * P]).then_inc(ident_ready, 1)

            def make_scales(c):
                own.tensor_scalar(mx_all[:, c], mx_all[:, c], 2.0 ** -40, None, ALU.max)
                dve.drain()
                bits = mx_all[:, c].bitcast(I32)
                own.tensor_scalar(bits, bits, 0x7F800000, None, ALU.bitwise_and)
                dve.drain()
                own.tensor_scalar(sc2[:, c].bitcast(I32), bits, -1.0, float((254 + 14) << 23), ALU.mult, ALU.add)
                dve.drain()
                own.reciprocal(inv2[:, c], sc2[:, c])
                dve.drain()

            def split(hi, lo, full, c):
                own.tensor_scalar(hi[:], full[:], sc2[:, c:c + 1], None, ALU.mult)
                dve.drain()
                own.scalar_tensor_tensor(lo[:], full[:], sc2[:, c:c + 1], hi[:], ALU.mult, ALU.subtract)

            def stats(b):
                dve.wait_ge(z_ready, b + 1)
                for i in range(T):
                    own.bn_stats(bst[:, i, :], h[:, b * T + i, :])
                dve.drain()
                for i in range(T):
                    own.bn_aggr(zmv[:, b * T + i, :], bst[:, i, :])
                dve.drain()

            def squares(q):
                c = cols_of(q)
                own.tensor_tensor(tmp[:, 0, c], zmv[:, c, 0], zmv[:, c, 0], ALU.mult)
                dve.drain()
                own.tensor_tensor(tmp[:, 0, c], tmp[:, 0, c], zmv[:, c, 1], ALU.add)
                if q == 0:
                    dve.wait_ge(scale_ready, 1)
                    own.tensor_tensor(th[:, 1:2], th[:, 0:1], th[:, 0:1], ALU.mult)
                dve.drain()
                own.tensor_scalar(tmp[:, 0, c], tmp[:, 0, c], th[:, 1:2], float(P), ALU.mult, ALU.mult)
                dve.drain().then_inc(sq_in, 1)

            def ball(q):
                c = cols_of(q)
                fb_, (t1, t2, t3, t4) = f[:, c], (tmp[:, k, c] for k in range(1, 5))
                dve.wait_ge(sq_ready, q + 1)
                own.tensor_scalar(t4, t1, MIN_NORM, None, ALU.max)
                dve.drain().then_inc(clamp_ready, 1)
                own.reciprocal(t3, t4)
                dve.wait_ge(tanh_ready, q + 1)
                dve.drain()
                own.tensor_tensor(t2, t2, t3, ALU.mult)
                dve.drain()
                own.tensor_tensor(fb_, t1, t2, ALU.mult)
                dve.drain()
                own.tensor_scalar(fb_, fb_, MIN_NORM, None, ALU.max)
                dve.drain()
                own.reciprocal(fb_, fb_)
                dve.drain()
                own.tensor_scalar(fb_, fb_, MAX_NORM, 1.0, ALU.mult, ALU.min)
                dve.drain()
                own.scalar_tensor_tensor(fb_, fb_, th[:, 0:1], t2, ALU.mult, ALU.mult)
                dve.drain()
                own.tensor_tensor(t3, fb_, fb_, ALU.mult)
                dve.drain()
                own.tensor_tensor(t3, t3, zmv[:, c, 1], ALU.mult)
                dve.drain()
                own.tensor_scalar(t3, t3, EPS_LN, None, ALU.add)
                dve.drain().then_inc(var1_ready, 1)

            def first_norm(b):
                q = [q for q, (a, _) in enumerate(SETS) if a == b]
                if q:
                    dve.wait_ge(inv1_ready, q[0] + 1)
                    c = cols_of(q[0])
                    own.tensor_tensor(frs[:, c], f[:, c], tmp[:, 4, c], ALU.mult)
                    dve.drain()
                    own.scalar_tensor_tensor(nmf[:, c], zmv[:, c, 0], -1.0, frs[:, c], ALU.mult, ALU.mult)
                    dve.drain().then_inc(nmf_ready, 1)
                if b:
                    dve.wait_ge(xT_mm, b)
                for i in range(ACT_TILES, T):
                    t = b * T + i
                    own.tensor_scalar(xn[:, i, :], h[:, t, :], zmv[:, t, 0:1], frs[:, t:t + 1],
                                      ALU.subtract, ALU.mult)
                dve.drain().then_inc(xn_ready, 1)

            def x_low(b):
                cols = slice(b * NP, (b + 1) * NP)
                dve.wait_ge(xTh_ready, b + 1)
                own.tensor_tensor(xTl[:, cols], banks(4, NP), xTh[:, cols], ALU.subtract).then_inc(xTl_ready, 1)

            def y_low(b):
                cols = slice(b * NP, (b + 1) * NP)
                dve.wait_ge(yh_ready, b + 1)
                own.tensor_tensor(yTl[:, cols].rearrange("p (k c) -> p k c", k=2), ps[:, 6:8, 0:NP // 2],
                                  yTh[:, cols].rearrange("p (k c) -> p k c", k=2), ALU.subtract)\
                   .then_inc(yl_ready, 1)

            def w_max(first, end):
                for k in range(first, end):
                    if k % E == 0:
                        dve.wait_ge(ld_w1 if k else ld_w2, 16)
                    k = (k + E) % NCH
                    own.reduce_max(mx_w[:, k:k + 1], raw[k], AX, apply_absolute_value=True)

            stats(0)
            squares(0)
            dve.wait_ge(filt_mm, 1)
            own.tensor_copy(cqk[:].rearrange("p a c -> p (a c)"), ps[:, 6, 0:2 * P]).then_inc(filt_cp, 1)
            own.tensor_copy(cv32[:], ps[:, 6, 2 * P:3 * P])
            stats(1)
            squares(1)
            ball(0)
            dve.wait_ge(filt_mm, 2)
            own.tensor_copy(g32[:], ps[:, 7, 0:P])
            dve.drain()
            own.reduce_max(mx_part[:, C_G:C_G + 1], g32[:], AX, apply_absolute_value=True)
            own.reduce_max(mx_part[:, C_V:C_V + 1], cv32[:], AX, apply_absolute_value=True)
            dve.wait_ge(ld_small, 3 * 16)
            own.reduce_max(mx_part[:, C_R:C_R + 1], wr_sb[:], AX, apply_absolute_value=True)
            dve.drain().then_inc(mx_ready, 1)
            stats(2)
            first_norm(0)
            stats(3)
            squares(2)
            ball(1)
            dve.wait_ge(mx_red, 1)
            own.tensor_scalar(mx_all[:, 0:C_1], mx_all[:, 0:C_1], float(P), None, ALU.mult)
            dve.drain()
            make_scales(slice(C_G, C_1))
            own.tensor_scalar(inv_s[:], inv2[:, C_G:C_G + 1], float(1.0 / np.sqrt(P).astype(np.float32)), None,
                              ALU.mult)
            split(gh, gl, g32, C_G)
            split(cvh, cvl, cv32, C_V)
            split(wrh, wrl, wr_sb, C_R)
            dve.drain().then_inc(splits_ready, 1)
            x_low(0)
            first_norm(1)
            ball(2)
            for b in range(B):
                if b + 1 < B:
                    x_low(b + 1)
                if b + 2 < B:
                    first_norm(b + 2)
                y_low(b)

            def row_max(t):
                u = t % 2
                dve.wait_ge(s_mm, t + 1)
                own.tensor_reduce(nmax[:, u:u + 1], ps[:, 2 * u:2 * u + 2, 0:KH], mybir.AxisListType.XY, ALU.max)

            def row_bias(t):
                u = t % 2
                own.tensor_scalar(nbias[:, u:u + 1], nmax[:, u:u + 1], inv_s[:], -1.0, ALU.mult, ALU.mult)\
                   .then_inc(nb_ready, 1)

            def bc(ap, n):
                return ap.unsqueeze(2).broadcast_to([P, n, E])

            def tiles_of(a, z):
                if z % T:
                    return [(P, a, z)]
                return [(P, a, z - 1), (LAST, z - 1, z)]

            dve.wait_ge(pool_c, 2)
            row_max(0)
            dve.drain()
            row_bias(0)
            for t in range(NSTEP):
                first, second = route_steps(t)
                if t + 1 < NT:
                    row_max(t + 1)
                m = t - 4
                if 0 <= m < NT:
                    dve.wait_ge(x2h_ready, m + 1)
                    own.tensor_tensor(halves(rowA)[:, m, P:2 * P], x2f[:, m % 2, :], halves(rowA)[:, m, 0:P],
                                      ALU.subtract).then_inc(x2l_ready, 1)
                if first:
                    dve.drain()
                for g in first:
                    a, z = GROUPS[g]
                    own.tensor_copy(ixf[:, a:z, :], ix8[:, a:z, 0:2])
                    own.tensor_tensor(gate[:, 0, a:z], top8[:, a:z, 1], top8[:, a:z, 0], ALU.subtract)
                for g in second:
                    a, z = GROUPS[g]
                    n = z - a
                    dve.wait_ge(e_ready, g + 1)
                    own.tensor_scalar(gate[:, 2, a:z], gate[:, 1, a:z], 1.0, None, ALU.add)
                    dve.wait_ge(pos_mm, g + 1)
                    own.tensor_tensor(posb[:, 0:n, :], ps[:, 7, P:P + n * E].rearrange("p (n e) -> p n e", e=E),
                                      ebase[:].unsqueeze(1).broadcast_to([P, n, E]), ALU.add)\
                       .then_inc(pos_used, 1)
                done = dve.drain()
                if first:
                    done.then_inc(d_ready, 1)
                if t + 1 < NT:
                    row_bias(t + 1)
                m = t - 2
                if 0 <= m < NT:
                    own.bn_aggr(h2mv[:, m, :], st6[:, m % 2, :])
                m = t - 3
                if 0 <= m < NT:
                    dve.wait_ge(rstd_ready, m + 1)
                    own.tensor_scalar(x2f[:, m % 2, :], h[:, m, :], h2mv[:, m, 0:1], rstd[:, m:m + 1],
                                      ALU.subtract, ALU.mult).then_inc(x2_ready, 1)
                m = t - TAIL
                if 0 <= m < NT:
                    dve.wait_ge(lg_ready, m + 1)
                    own.max(top8[:, m, :], lg[:, m, :])
                m = t - 1
                if 0 <= m < NT:
                    dve.wait_ge(o_mm, m + 1)
                    if m % T == 0:
                        dve.wait_ge(h_ready, m // T + 1)
                    own.scalar_tensor_tensor(h[:, m, :], ps[:, 6, 0:P], rinv[:, m % 2:m % 2 + 1], h[:, m, :],
                                             ALU.mult, ALU.add).then_inc(o_used, 1)
                if t < NT:
                    dve.wait_ge(p_ready, t + 1)
                    own.reciprocal(rinv[:, t % 2:t % 2 + 1], rsum[:, t % 2:t % 2 + 1])
                for g in first:
                    a, z = GROUPS[g]
                    sh = [P, 2, z - a, E]
                    own.tensor_tensor(m12[:, :, a:z, :], iota8[:].unsqueeze(1).unsqueeze(1).broadcast_to(sh),
                                      ixf[:, a:z, :].rearrange("p t k -> p k t").unsqueeze(3).broadcast_to(sh),
                                      ALU.is_equal)
                for g in second:
                    a, z = GROUPS[g]
                    own.tensor_tensor(q12[:, :, 0:z - a, :], m12[:, :, a:z, :],
                                      posb[:, 0:z - a, :].unsqueeze(1).broadcast_to([P, 2, z - a, E]), ALU.mult)
                    own.reciprocal(rowA[:, a:z, P], gate[:, 2, a:z])
                dve.drain()
                m = t - 2
                if 0 <= m < NT:
                    own.tensor_scalar(veps[:, m:m + 1], h2mv[:, m, 1:2], EPS_LN, None, ALU.add)\
                       .then_inc(var_ready, 1)
                m = t - 1
                if 0 <= m < NT:
                    own.bn_stats(st6[:, m % 2, :], h[:, m, :])
                m = t - TAIL
                if 0 <= m < NT:
                    own.max_index(ix8[:, m, :], top8[:, m, :], lg[:, m, :])
                for g in first:
                    a, z = GROUPS[g]
                    for rows_, a_, z_ in tiles_of(a, z):
                        own.tensor_tensor(mh[0:rows_, a_:z_, :], m12[0:rows_, 0, a_:z_, :],
                                          m12[0:rows_, 1, a_:z_, :], ALU.add)
                    dve.drain().then_inc(m_ready, 1)
                    own.tensor_reduce(hist[:, g, :], mh[:, a:z, :].rearrange("p t e -> p e t"), AX, ALU.add)
                    dve.drain()
                    own.tensor_tensor(seen[:, g + 1, :], seen[:, g, :], hist[:, g, :], ALU.add)
                for g in second:
                    a, z = GROUPS[g]
                    own.tensor_tensor(rowB[:, a:z, P], gate[:, 1, a:z], rowA[:, a:z, P], ALU.mult)
                    own.tensor_reduce(slotf[:, :, 0:z - a], q12[:, :, 0:z - a, :], AX, ALU.add)
                    dve.drain()
                    for rows_, a_, z_ in tiles_of(a, z):
                        own.tensor_copy(slot[0:rows_, :, a_:z_], slotf[0:rows_, :, a_ - a:z_ - a])
                    dve.drain().then_inc(slot_ready, 1)
                if t < W_MAX - 1:
                    w_max(2 * t, 2 * t + 2)
                if t == W_MAX - 1:
                    own.reduce_max(mx_part[:, C_1:C_1 + 1], mx_w[:, 0:E], AX)
                    own.reduce_max(mx_part[:, C_2:C_2 + 1], mx_w[:, E:], AX)
                    own.reduce_max(mx_part[:, C_B:C_B + 1], b1_sb[:], AX, apply_absolute_value=True)
                    dve.drain().then_inc(mx_ready, 1)
                if t == W_SCALE:
                    dve.wait_ge(mx_red, 2)
                    own.tensor_scalar(mx_all[:, C_1:C_1 + 1], mx_all[:, C_1:C_1 + 1], float(P), None, ALU.mult)
                    dve.drain()
                    own.tensor_tensor(mx_all[:, C_1:C_1 + 1], mx_all[:, C_1:C_1 + 1], mx_all[:, C_B:C_B + 1],
                                      ALU.max)
                    dve.drain()
                    make_scales(slice(C_1, C_B))
                    own.tensor_tensor(inv12[:], inv2[:, C_1:C_1 + 1], inv2[:, C_2:C_2 + 1], ALU.mult)
                    own.tensor_tensor(sc12[:], sc2[:, C_1:C_1 + 1], sc2[:, C_2:C_2 + 1], ALU.mult)
                    own.tensor_scalar(nb1[:], b1_sb[:], sc2[:, C_1:C_1 + 1], -1.0, ALU.mult, ALU.mult)
                    dve.drain().then_inc(w_scaled, 1)
                if t == W_SCALE + 1:
                    own.tensor_copy(nb1h[:], nb1[:])
                    dve.drain()
                    own.tensor_tensor(nb1l[:], nb1[:], nb1h[:], ALU.subtract)
                k = t - W_SPLIT0 - 1
                if 0 <= k < NCH:
                    c = C_1 if k < E else C_2
                    dve.wait_ge(wh_ready, k + 1)
                    own.scalar_tensor_tensor(w_lo[k], raw[k], sc2[:, c:c + 1], w_hi[k], ALU.mult,
                                             ALU.subtract).then_inc(wl_ready, 1)
            dve.wait_ge(cnt_mm, 1)
            cnt = ps[:, 6, 0:E]
            own.tensor_scalar(cnti[:], cnt, float(S - 1), None, ALU.add)
            own.tensor_tensor(tab_pad[:], cnt, ebase[:], ALU.add)
            dve.drain().then_inc(cnt_ready, 1)
            own.tensor_scalar(ntli[:], cnti[:], S.bit_length() - 1, None, ALU.logical_shift_right)
            dve.drain()
            own.tensor_copy(ntl[:], ntli[:])
            dve.drain()
            own.tensor_tensor_scan(cum[:], one8[:], ntl[:], 0.0, ALU.mult, ALU.add)
            dve.drain()
            n_e = [P, NS, E]
            own.tensor_tensor(past[:], cum[:].unsqueeze(1).broadcast_to(n_e),
                              stepno[:].unsqueeze(2).broadcast_to(n_e), ALU.is_le)
            dve.drain()
            own.reduce_sum(ej[:], past[:], AX)
            own.tensor_tensor(pastn[:], past[:], ntl[:].unsqueeze(1).broadcast_to(n_e), ALU.mult)
            dve.drain()
            own.reduce_sum(sj[:], pastn[:], AX)
            own.tensor_scalar(step_e[:, 0:NS], ej[:], float(E - 1), None, ALU.min)
            dve.drain()
            own.tensor_copy(tab_e[:], step_e[:])
            own.tensor_tensor(packed[:],
                              step_e[:, 2:2 + PACK * ((NS - 1) // PACK)].rearrange("p (a k) -> p a k", k=PACK),
                              pow8[:].unsqueeze(1).broadcast_to([P, (NS - 1) // PACK, PACK]), ALU.mult)
            own.tensor_tensor(sj[:], stepno[:], sj[:], ALU.subtract)
            own.tensor_scalar(ej[:], ej[:], float(R), None, ALU.mult)
            dve.drain()
            own.reduce_sum(packf[:], packed[:], AX)
            own.scalar_tensor_tensor(sj[:], sj[:], float(S), ej[:], ALU.mult, ALU.add)
            dve.drain()
            own.tensor_copy(tab_pack[:], packf[:])
            own.tensor_scalar(tab_row[:], sj[:], float(DUMMY), None, ALU.min)
            dve.drain().then_inc(table_ready, 1)
            own.tensor_tensor(onehot[:], iota8[:].unsqueeze(1).broadcast_to(n_e),
                              step_e[:, 0:NS].unsqueeze(2).broadcast_to(n_e), ALU.is_equal)
            dve.drain()
            for c in range(HC):
                own.tensor_tensor(nbp[:, :, c, :], onehot[:],
                                  nb1[:].rearrange("p (e c) -> p c e", c=HC)[:, c, :].unsqueeze(1).broadcast_to(n_e),
                                  ALU.mult)
            dve.drain()
            own.reduce_sum(nbs[:, 0:NS, :], nbp[:], AX)
            dve.drain()
            own.tensor_scalar(cc[:], b2_sb[:], sc12[:], None, ALU.mult)
            dve.wait_ge(c_mm, 1)
            dve.drain()
            own.tensor_tensor(cc[:], cc[:], ps[:, 1, 0:E], ALU.subtract)
            dve.drain()
            for part in range(3):
                own.tensor_copy(cbf[:, part, :], cc[:])
                dve.drain()
                own.tensor_copy(c24[:, part, :], cbf[:, part, :])
                own.tensor_tensor(cc[:], cc[:], cbf[:, part, :], ALU.subtract)
                dve.drain()
            dve.drain().then_inc(c24_ready, 1)
            dve.wait_ge(c3_mm, 1)
            own.tensor_copy(c3[0:3 * E, :], ps[0:3 * E, 0, 0:P])
            dve.drain().then_inc(c3_ready, 1)

            def hidden(i, u, at):
                n = RING * i + u
                for q in range(2):
                    dve.wait_ge(h_mm, 2 * n + q + 1)
                    own.tensor_tensor(
                        hu[:, u % 2, q * 2 * S:(q + 1) * 2 * S].rearrange("p (c n) -> p c n", c=2),
                        ps[:, 2 * (u % 2) + q, :].rearrange("p (c n) -> p c n", c=2),
                        nbs[:, at, 2 * q:2 * q + 2].rearrange("p a c -> p (a c)").unsqueeze(2)
                        .broadcast_to([P, 2, S]),
                        ALU.max).then_inc(hu_ready, 1)

            def low(i, u):
                n = RING * i + u
                for q in range(2):
                    c = slice(q * 2 * S, (q + 1) * 2 * S)
                    dve.wait_ge(huh_ready, 2 * n + q + 1)
                    own.tensor_tensor(hul[:, u % 2, c], hu[:, u % 2, c], huh[:, u % 2, c], ALU.subtract)\
                       .then_inc(hul_ready, 1)

            def take_meta(i, u):
                n = RING * i + u
                dve.wait_ge(xin_ready[u % RING], 16 * (i + u // RING) + 16)
                dve.wait_ge(yb_free[u % RING], 32 * (i + u // RING) + 16)
                own.tensor_copy(ixy[:, u % RING, :], xin[:, u % RING, :, ROW - 1]).then_inc(ix_ready, 1)
                own.tensor_scalar(wy[:, u % RING, :], xin[:, u % RING, :, P], inv12[:], None, ALU.mult)\
                   .then_inc(wy_ready, 1)

            take_meta(0, 0)
            hidden(0, 0, slice(0, 1))
            low(0, 0)
            hidden(0, 1, slice(1, 2))
            take_meta(0, 1)
            low(0, 1)
            with dve.Fori(0, (NS - 1) // RING) as i:
                for u in range(1, RING + 1):
                    n = RING * i + u
                    hidden(i, u + 1, bass.ds(n + 1, 1))
                    take_meta(i, u + 1)
                    low(i, u + 1)

            for b in range(B):
                dve.wait_ge(yin_ready[b], 32)
                parts = ((slice(0, P), slice(0, T - 1)), (slice(0, LAST), slice(T - 1, T)))
                for k in range(2):
                    for p_, i_ in parts:
                        hb = h[p_, b * T + i_.start:b * T + i_.stop, :]
                        own.tensor_tensor(hb, hb, yin[b][p_, i_, k, :], ALU.add)
                    dve.drain()
                dve.drain().then_inc(out_ready, 1)

        @block.tensor
        def _(pe):
            mm = nc.tensor.matmul

            def three(out_ap, lhs, rhs):
                (lh, ll), (rh, rl) = lhs, rhs
                mm(out_ap, lh, rh, start=True, stop=False)
                mm(out_ap, lh, rl, start=False, stop=False)
                return mm(out_ap, ll, rh, start=False, stop=True)

            def windows(b):
                pe.wait_ge(ld_seg[b], 32)
                if b >= 2:
                    pe.wait_ge(segT_ready, b - 1)
                for i in range(T):
                    last = nc.tensor.transpose(banks(4 * (b % 2), NP)[0:K, i * P:(i + 1) * P], seg[:, b, i, :],
                                               ident)
                last.then_inc(segT_mm, 1)

            def tokenise(b):
                pe.wait_ge(segT_ready, b + 1)
                if b:
                    pe.wait_ge(z_ready, b)
                for i in range(T):
                    last = mm(banks(2, NP)[:, i * P:(i + 1) * P], segT[:, b % 2, i * P:(i + 1) * P], wb_sb[:],
                              start=True, stop=True)
                last.then_inc(z_mm, 1)

            def turn_x(b):
                pe.wait_ge(xn_ready, b + 1)
                pe.wait_ge(xa_ready, ACT_TILES * (b + 1))
                if b:
                    pe.wait_ge(xTl_ready, b)
                for i in range(T):
                    last = nc.tensor.transpose(banks(4, NP)[:, i * P:(i + 1) * P], xn[:, i, :], ident)
                last.then_inc(xT_mm, 1)

            def qk(b):
                pe.wait_ge(xTl_ready, b + 1)
                if b:
                    pe.wait_ge(yl_ready, b)
                for k in range(2):
                    cols = slice(b * NP + k * (NP // 2), b * NP + (k + 1) * (NP // 2))
                    last = three(ps[:, 6 + k, 0:NP // 2], (gh[:], gl[:]), (xTh[:, cols], xTl[:, cols]))
                last.then_inc(y_mm, 1)

            def values(b):
                if b:
                    pe.wait_ge(v_ready, b)
                for i in range(T):
                    cols = slice(b * NP + i * P, b * NP + (i + 1) * P)
                    last = three(banks(0, NP)[:, i * P:(i + 1) * P], (xTh[:, cols], xTl[:, cols]),
                                 (cvh[:], cvl[:]))
                last.then_inc(v_mm, 1)

            pe.wait_ge(ones_seg, 1)
            pe.wait_ge(ld_tab, 16)
            windows(0)
            windows(1)
            pe.wait_ge(ld_wb, 32)
            tokenise(0)
            pe.wait_ge(filt_ready, 1)
            for q in range(2):
                mm(ps[:, 6, q * P:q * P + P], fa[:, q, :], cos_t, start=True, stop=False)
                mm(ps[:, 6, q * P:q * P + P], fb[:, q, :], sin_t, start=False, stop=True)
            mm(ps[:, 6, 2 * P:3 * P], cos_t, fa[:, 2, :], start=True, stop=False)
            mm(ps[:, 6, 2 * P:3 * P], sin_t, fb[:, 2, :], start=False, stop=True).then_inc(filt_mm, 1)
            windows(2)
            tokenise(1)
            pe.wait_ge(filt_cp, 1)
            mm(ps[:, 7, 0:P], cqk[:, 0, :], cqk[:, 1, :], start=True, stop=True).then_inc(filt_mm, 1)
            windows(3)
            tokenise(2)
            tokenise(3)
            pe.wait_ge(segT_ready, B)
            pe.wait_ge(z_ready, B)
            turn_x(0)
            pe.wait_ge(splits_ready, 1)
            turn_x(1)
            qk(0)
            values(0)
            for b in range(1, B):
                if b + 1 < B:
                    turn_x(b + 1)
                qk(b)
                values(b)
            pe.wait_ge(pool_c, 2)
            pe.wait_ge(ident_ready, 1)
            pe.wait_ge(yl_ready, B)
            pe.wait_ge(v_ready, B)

            def scores(t):
                b, u = t // T, t % 2
                q = slice(t * P, (t + 1) * P)
                for k in range(2):
                    keys = slice(b * NP + k * KH, b * NP + (k + 1) * KH)
                    last = three(ps[:, 2 * u + k, 0:KH], (yTh[:, q], yTl[:, q]), (xTh[:, keys], xTl[:, keys]))
                last.then_inc(s_mm, 1)

            scores(0)
            scores(1)
            for t in range(NSTEP):
                b, u = t // T, t % 2
                if t < NT:
                    pe.wait_ge(p_ready, t + 1)
                    if t >= 1:
                        pe.wait_ge(pT_ready, t)
                    if t >= 6:
                        pe.wait_ge(lg_ready, t - 5)
                    for i in range(T):
                        last = nc.tensor.transpose(banks(4, NP)[:, i * P:(i + 1) * P],
                                                   prob[:, u, i * P:(i + 1) * P], ident)
                    last.then_inc(pT_mm, 1)
                for g in route_steps(t)[1]:
                    a, z = GROUPS[g]
                    n = z - a
                    pe.wait_ge(m_ready, g + 1)
                    if t - 5 < NT:
                        pe.wait_ge(x2T_ready, t - 4)
                    pos = ps[:, 7, P:P + n * E].rearrange("p (n e) -> p n e", e=E)
                    mm(pos, trib[:], mh[:, a:z, :], start=True, stop=False)
                    for j in range(1, n):
                        mm(pos[:, j:, :], ones[:], mh[:, a + j - 1:a + j, :].broadcast_to([P, n - j, E]),
                           start=False, stop=False)
                    mm(pos, ones[:], seen[:, g:g + 1, :].broadcast_to([P, n, E]), start=False, stop=True)\
                        .then_inc(pos_mm, 1)
                if t + 2 < NT:
                    scores(t + 2)
                m = t - 4
                if 0 <= m < NT:
                    pe.wait_ge(x2l_ready, m + 1)
                    if m >= 1:
                        pe.wait_ge(x2T_ready, m)
                    for g in route_steps(t)[1]:
                        pe.wait_ge(pos_used, g + 1)
                    for k in range(2):
                        last = nc.tensor.transpose(ps[:, 7, 0:P].bitcast(F16)[:, k * P:(k + 1) * P],
                                                   halves(rowA)[:, m, k * P:(k + 1) * P], identh[:])
                    last.then_inc(x2T_mm, 1)
                m = t - 5
                if 0 <= m < NT:
                    pe.wait_ge(x2T_ready, m + 1)
                    if t < NT:
                        pe.wait_ge(pT_ready, t + 1)
                    elif m >= 1:
                        pe.wait_ge(lg_ready, m)
                    x2 = x2T[:, m % 2, :]
                    three(ps[:, 5, NP - 512:NP - 512 + E], (x2[:, 0:P], x2[:, P:2 * P]), (wrh[:], wrl[:]))\
                        .then_inc(lg_mm, 1)
                if t < NT:
                    if t >= 1:
                        pe.wait_ge(o_used, t)
                    pe.wait_ge(pT_ready, t + 1)
                    for i in range(T):
                        last = mm(ps[:, 6, 0:P], probT[:, u, i * P:(i + 1) * P], v32[:, b * T + i, :],
                                  start=(i == 0), stop=(i == T - 1))
                    last.then_inc(o_mm, 1)
            pe.wait_ge(slot_ready, NGR)
            mm(ps[:, 6, 0:E], ones[:], seen[:, NGR, :], start=True, stop=True).then_inc(cnt_mm, 1)
            pe.wait_ge(wl_ready, NCH)
            for e in range(E):
                for c in range(HC):
                    k, cols = e * HC + c, slice(c * P, (c + 1) * P)
                    for w_, b_ in ((w_hi, nb1h), (w_hi, nb1l), (w_lo, nb1h)):
                        last = mm(ps[:, 1, e:e + 1], w_[E + e][:, cols], b_[:, k:k + 1],
                                  start=(c == 0 and b_ is nb1h and w_ is w_hi), stop=(c == HC - 1 and w_ is w_lo))
            last.then_inc(c_mm, 1)
            pe.wait_ge(c24_ready, 1)
            nc.tensor.transpose(ps[0:3 * E, 0, 0:P], c24[:].rearrange("p a e -> p (a e)"), ident)\
                .then_inc(c3_mm, 1)

            def turn(i, u):
                n = RING * i + u
                pe.wait_ge(xin_ready[u % RING], 16 * (i + u // RING) + 16)
                for q in range(2):
                    for j in range(2):
                        last = nc.tensor.transpose(
                            ps[:, 4 + u % 2, 0:S].bitcast(F16)[:, q * S + j * P:q * S + (j + 1) * P],
                            xin[:, u % RING, j, 0:P].bitcast(F16)[:, q * P:(q + 1) * P], identh[:])
                last.then_inc(xe_mm, 1)

            def weights_at(e, chunk):
                return e * (2 * WC) + chunk * 2 * WC

            def expert_of(n):
                return pe.value_load(tab_e[0:1, n], min_val=0, max_val=E - 1)

            def up(i, u, e):
                n = RING * i + u
                pe.wait_ge(xe_ready, n + 1)
                xh, xl = xeT[:, u % 2, 0:S], xeT[:, u % 2, S:2 * S]
                for c in range(HC):
                    w = weights_at(e, 0) + c * P
                    last = three(ps[:, 2 * (u % 2) + c // 2, (c % 2) * S:(c % 2 + 1) * S],
                                 (wall16[:, bass.ds(w, P)], wall16[:, bass.ds(w + WC, P)]), (xh, xl))
                    if c % 2:
                        last.then_inc(h_mm, 1)

            pick_cols = pick[:].rearrange("p e c -> p (e c)")

            def down(i, u, e):
                n = RING * i + u
                y = [ps[:, 6 + u % 2, j * P:(j + 1) * P] for j in range(2)]
                mm(ps[:, 6 + u % 2, 0:S].rearrange("p (j c) -> p j c", j=2), pick_cols[:, bass.ds(e * P, P)],
                   c3[:].unsqueeze(1).broadcast_to([P, 2, P]), start=True, stop=False)
                for c in range(HC):
                    if c % 2 == 0:
                        pe.wait_ge(huh_ready, 2 * n + c // 2 + 1)
                        pe.wait_ge(hul_ready, 2 * n + c // 2 + 1)
                    w = weights_at(e, E) + c * P
                    whi, wlo = wall16[:, bass.ds(w, P)], wall16[:, bass.ds(w + WC, P)]
                    for j in range(2):
                        hid = slice(c * S + j * P, c * S + (j + 1) * P)
                        mm(y[j], huh[:, u % 2, hid], whi, start=False, stop=False)
                        mm(y[j], hul[:, u % 2, hid], whi, start=False, stop=False)
                    for j in range(2):
                        hid = slice(c * S + j * P, c * S + (j + 1) * P)
                        last = mm(y[j], huh[:, u % 2, hid], wlo, start=False, stop=(c == HC - 1 and j == 1))
                last.then_inc(e_mm, 1)

            pe.wait_ge(table_ready, 1)
            pe.wait_ge(wl_ready, NCH)
            pe.wait_ge(c3_ready, 1)
            pe.wait_ge(pick_ready, 1)
            e0, e1 = expert_of(slice(0, 1)), expert_of(slice(1, 2))
            turn(0, 0)
            turn(0, 1)
            up(0, 0, e0)
            turn(0, 2)
            up(0, 1, e1)
            down(0, 0, e0)
            with pe.Fori(0, (NS - 1) // PACK) as i2:
                i = (PACK // RING) * i2
                word = pe.value_load(tab_pack[0:1, bass.ds(i2, 1)], min_val=0, max_val=E ** PACK - 1)
                e_down = expert_of(bass.ds(PACK * i2 + 1, 1))
                for u in range(1, PACK + 1):
                    e_up = (word >> (3 * (u - 1))) & (E - 1)
                    turn(i, u + 2)
                    up(i, u + 1, e_up)
                    down(i, u, e_down)
                    e_down = e_up

def _tables():
    k = np.arange(P)
    a = 2 * np.pi * ((k[:, None] * k[None, :]) % P) / P
    tri = (k[:, None] < k[None, :]).astype(np.float64)
    return np.concatenate([np.cos(a), np.sin(a), np.eye(P), tri], 1).astype(np.float32)

def kernel(**inputs):
    import concourse.bacc as bacc
    from concourse.bass_utils import run_bass_kernel_spmd

    a = {k: np.ascontiguousarray(v) for k, v in inputs.items()}
    ins = {
        "x": a["x"],
        "wb": np.concatenate([a["L0_tok_W"], a["L0_tok_b"][None]], 0),
        "scale": np.repeat(a["L0_tok_effective_scale"][None], P, 0),
        "tables": _tables(),
        "filters": np.stack([a["L0_attn_" + n] for n in (
            "q_real", "q_imag", "k_real", "k_imag", "v_real", "v_imag")], 1),
        "wr": a["L0_ffn_W_router"],
        "w1": np.ascontiguousarray(a["L0_ffn_W1"].transpose(1, 0, 2).reshape(P, E * H)),
        "b1t": np.ascontiguousarray(a["L0_ffn_b1"].reshape(E * HC, P).T),
        "w2": np.ascontiguousarray(a["L0_ffn_W2"].reshape(E * HC, P, P).transpose(1, 0, 2).reshape(P, E * H)),
        "b2": a["L0_ffn_b2"].T,
    }
    ins = {k: np.ascontiguousarray(v) for k, v in ins.items()}
    nc = bacc.Bacc("TRN2", target_bir_lowering=False, num_devices=1)
    aps = [nc.dram_tensor("in_" + k, v.shape, F32, kind="ExternalInput").ap() for k, v in ins.items()]
    out = nc.dram_tensor("out", (B, N, P), F32, kind="ExternalOutput").ap()
    build(nc, *aps, out)
    r = run_bass_kernel_spmd(nc, [{"in_" + k: v for k, v in ins.items()}], core_ids=[0])
    return r.results[0]["out"]
```
